# Optimizing a Trainium2 kernel written in Bass

```python
import numpy as np
import jax
import jax.numpy as jnp

def _softmax(x, axis=-1):
    return jax.nn.softmax(x, axis=axis)

def _gelu(x):
    return jax.nn.gelu(x, approximate=True)

def _silu(x):
    return jax.nn.silu(x)

def _sigmoid(x):
    return jax.nn.sigmoid(x)

def _layernorm(x, axis=-1, eps=1e-05):
    m = jnp.mean(x, axis=axis, keepdims=True)
    v = jnp.var(x, axis=axis, keepdims=True)
    return (x - m) / jnp.sqrt(v + eps)

def _scatter_add(tgt, idx, src, axis=0):
    return tgt.at[idx].add(src)

def _segment_sum(src, seg, n):
    return jax.ops.segment_sum(src, seg, n)
kernel_name = 'mk_adj_resnorm_d2_adj_r2_f09700'

def setup_inputs(seed: int=0):
    np.random.seed(seed)
    _w = jnp.asarray

    def _rec_inputs():
        import jax
        import jax.numpy as jnp
        _gk = jax.random.key(seed)
        x = -0.0005207 + 1.001 * jax.random.normal(jax.random.fold_in(_gk, 1), (4096, 128), jnp.float32)
        _a = jax.random.bernoulli(jax.random.fold_in(_gk, 2), 0.000976562, (4096, 4096))
        _a = jnp.logical_or(_a, jnp.eye(4096, dtype=bool))
        _af = _a.astype(jnp.float32)
        _af = _af * jax.random.uniform(jax.random.fold_in(_gk, 3), (4096, 4096), jnp.float32, 0.05, 1)
        adj = _af
        return (x, adj)
    x, adj = _rec_inputs()

    def _L0_gnn_setup():
        import jax, jax.numpy as jnp
        import numpy as np
        N = 4096
        D = 128
        L = 3

        def _cxin_conv(x, a, eps, W, b):
            ax = a @ x
            h = ax + (1.0 + eps[0]) * ax
            for i in range(L):
                h = jax.nn.relu(h @ W[i].T + b[i])
            return h
        key = jax.random.key(seed)
        ks = jax.random.split(key, 8)
        s = 1.0 / np.sqrt(D)
        return {'x1': jax.random.normal(ks[0], (N, D), jnp.float32), 'x2': jax.random.normal(ks[1], (N, D), jnp.float32), 'G1': jax.random.uniform(ks[2], (N, N), jnp.float32), 'G2': jax.random.uniform(ks[3], (N, N), jnp.float32), 'eps1': jnp.zeros((1,), jnp.float32), 'eps2': jnp.zeros((1,), jnp.float32), 'W1': jax.random.normal(ks[4], (L, D, D), jnp.float32) * s, 'b1': jnp.zeros((L, D), jnp.float32), 'W2': jax.random.normal(ks[5], (L, D, D), jnp.float32) * s, 'b2': jnp.zeros((L, D), jnp.float32), 'Wm': jax.random.normal(ks[6], (D, 2 * D), jnp.float32) * (1.0 / np.sqrt(2 * D)), 'bm': jnp.zeros((D,), jnp.float32)}
    _L0_gnn_all = _L0_gnn_setup()
    _L0_gnn_in = {k: v for k, v in _L0_gnn_all.items() if k in ('x2', 'eps1', 'eps2', 'W1', 'b1', 'W2', 'b2', 'Wm', 'bm')}
    del _L0_gnn_all

    def _L1_gnn_setup():
        import jax, jax.numpy as jnp
        import numpy as np
        key = jax.random.key(seed)
        k1, k2, k3, k4 = jax.random.split(key, 4)
        N, F_in, F_out = (4096, 128, 128)
        x = jax.random.normal(k1, (N, F_in), dtype=jnp.float32)
        adj = jax.random.uniform(k2, (N, N), dtype=jnp.float32)
        lim = 1.0 / np.sqrt(F_in)
        W = jax.random.uniform(k3, (F_out, F_in), dtype=jnp.float32, minval=-lim, maxval=lim)
        b = jax.random.uniform(k4, (F_out,), dtype=jnp.float32, minval=-lim, maxval=lim)
        return {'x': x, 'adj': adj, 'W': W, 'b': b}
    _L1_gnn_all = _L1_gnn_setup()
    _L1_gnn_in = {k: v for k, v in _L1_gnn_all.items() if k in ('W', 'b')}
    del _L1_gnn_all
    return {'x': x, 'adj': adj, 'L0_gnn_x2': _L0_gnn_in['x2'], 'L0_gnn_eps1': _L0_gnn_in['eps1'], 'L0_gnn_eps2': _L0_gnn_in['eps2'], 'L0_gnn_W1': _L0_gnn_in['W1'], 'L0_gnn_b1': _L0_gnn_in['b1'], 'L0_gnn_W2': _L0_gnn_in['W2'], 'L0_gnn_b2': _L0_gnn_in['b2'], 'L0_gnn_Wm': _L0_gnn_in['Wm'], 'L0_gnn_bm': _L0_gnn_in['bm'], 'L1_gnn_W': _L1_gnn_in['W'], 'L1_gnn_b': _L1_gnn_in['b']}

def reference(x, adj, L0_gnn_x2, L0_gnn_eps1, L0_gnn_eps2, L0_gnn_W1, L0_gnn_b1, L0_gnn_W2, L0_gnn_b2, L0_gnn_Wm, L0_gnn_bm, L1_gnn_W, L1_gnn_b):
    import jax
    import jax.numpy as jnp

    def _L0_gnn_ref(x1, x2, G1, G2, eps1, eps2, W1, b1, W2, b2, Wm, bm):
        import jax, jax.numpy as jnp
        import numpy as np
        N = 4096
        D = 128
        L = 3

        def _cxin_conv(x, a, eps, W, b):
            ax = a @ x
            h = ax + (1.0 + eps[0]) * ax
            for i in range(L):
                h = jax.nn.relu(h @ W[i].T + b[i])
            return h
        out1 = _cxin_conv(x1, G1, eps1, W1, b1)
        out2 = _cxin_conv(x2, G2, eps2, W2, b2)
        merged = jnp.concatenate((out1, out2), axis=1)
        return merged @ Wm.T + bm

    def _L1_gnn_ref(x, adj, W, b):
        import jax, jax.numpy as jnp
        import numpy as np
        N = adj.shape[0]
        adj = adj + jnp.eye(N, dtype=adj.dtype)
        deg = adj.sum(axis=1)
        deg_inv_sqrt = deg ** (-0.5)
        deg_inv_sqrt = jnp.where(jnp.isinf(deg_inv_sqrt), 0.0, deg_inv_sqrt)
        adj_normalized = deg_inv_sqrt[:, None] * adj * deg_inv_sqrt[None, :]
        support = x @ W.T + b
        return adj_normalized @ support
    x = _layernorm(x + _L0_gnn_ref(x, L0_gnn_x2, adj, adj, L0_gnn_eps1, L0_gnn_eps2, L0_gnn_W1, L0_gnn_b1, L0_gnn_W2, L0_gnn_b2, L0_gnn_Wm, L0_gnn_bm), axis=-1)
    x = _layernorm(x + _L1_gnn_ref(x, adj, L1_gnn_W, L1_gnn_b), axis=-1)
    return x

_drawn_inputs = setup_inputs


def setup_inputs(seed=0):
    import zlib

    import numpy as np

    out = dict(_drawn_inputs(seed))
    spreads = {'L0_gnn_b1': (0.0, 0.1), 'L0_gnn_b2': (0.0, 0.1), 'L0_gnn_bm': (0.0, 0.1)}
    factors = {}
    for name, (base, spread) in spreads.items():
        noise = np.random.default_rng([zlib.crc32(name.encode()), seed]).standard_normal(out[name].shape)
        drawn = base * np.exp(spread * noise) if base else spread * noise
        out[name] = jnp.asarray(drawn.astype(out[name].dtype))
    for name, factor in factors.items():
        out[name] = (out[name] * factor).astype(out[name].dtype)
    return out
```

```python
from contextlib import ExitStack

import concourse.bass as bass
from concourse import mybir

F32 = mybir.dt.float32
F32R = mybir.dt.float32r
ALU = mybir.AluOpType
ACT = mybir.ActivationFunctionType
AX = mybir.AxisListType

P = 128
LN_EPS = 1e-5
LAYERS = 3

ORDER = [(0, q) for q in range(6)] + [(1, q) for q in range(6)] + [(0, 6), (0, 7), (1, 6), (1, 7)]
KIND = ["P", "F", "P", "D", "P", "F", "P", "P"]
KINDS = [KIND[q] for _, q in ORDER]
PLAIN = [q for q in range(8) if KIND[q] == "F"]
UNITS = [ORDER[p] for p in range(0, len(ORDER), 2)]


def program(nc, x, adj, x2, eps1, eps2, W1, b1, W2, b2, Wm, bm, W, b, out, y_dram):
    N, D = x.shape
    G = 16
    CH = N // (32 * G)
    TB = 4
    UN = CH // 2
    UC = N // UN // 4
    QS = range(CH)
    PAIRS = CH // 2
    TILES = CH * CH
    assert D == P and UC == 256

    A_v = adj.rearrange("(u g h i) (v a k) -> u h v a i g k", u=UN, g=G, h=2, i=32, v=UN, a=4)
    x_stage = [t.rearrange("(v a t j) d -> v a j t d", v=UN, a=4, t=8, j=32) for t in (x, x2)]
    y_v = y_dram.rearrange("(u a b h j) d -> u h a j b d", u=UN, a=4, b=TB, h=2, j=32)
    out_v = out.rearrange("(u a b h j) d -> u h a j b d", u=UN, a=4, b=TB, h=2, j=32)

    with ExitStack() as ctx:
        def sb(name, shape, dt=F32, c=ctx):
            return c.enter_context(nc.sbuf_tensor(name, shape, dt))

        def sem(name):
            return ctx.enter_context(nc.semaphore(name))

        Sh = sb("S_hi", [P, CH, TB, D], F32R)
        Sl = sb("S_lo", [P, CH, TB, D], F32R)
        S32 = sb("S_plain", [P, 2, TB, D])
        hid = sb("hidden", [P, 2, TB * P])
        WT = sb("weights_T", [P, 9, P])
        ident = sb("ident", [P, P])
        quad_sum = sb("quad_sum", [P, P])
        bm_row = sb("bm_row", [P, D])
        b_row = sb("b_row", [P, D])
        bT = sb("bias_T", [P, 2 * LAYERS])
        ax_scale = sb("ax_scale", [P, 2])
        deg_part = sb("deg_part", [P, UN, G])
        deg_quad = sb("deg_quad", [P, G])
        deg = sb("deg", [P, TB])
        deg_zero = sb("deg_zero", [P, TB])
        deg_pow = sb("deg_pow", [P, TB])
        dinv = sb("dinv", [P, TB])
        dinv_all = sb("dinv_all", [P, CH, TB])
        stats = sb("stats", [P, TB, 6])
        mean = sb("mean", [P, TB])
        mean_diff = sb("mean_diff", [P, TB])
        var_eps = sb("var_eps", [P, TB])
        rstd = sb("rstd", [P, TB])
        minus_half = sb("minus_half", [P, TB])
        R = sb("A_rows", [P, 2, G, UC])
        T = sb("A_cols", [P, 4, TB, G, 32])
        H = sb("A_hi", [P, 2, TB, G * 32], F32R)
        L = sb("A_lo", [P, 2, TB, G * 32], F32R)
        with ExitStack() as first:
            Xh1 = sb("x_hi", [P, CH, TB, D], F32R, first)
            Xl1 = sb("x_lo", [P, CH, TB, D], F32R, first)
            Xh2 = sb("x2_hi", [P, CH, TB, D], F32R, first)
            Xl2 = sb("x2_lo", [P, CH, TB, D], F32R, first)
        Xh, Xl = (Xh1, Xh2), (Xl1, Xl2)
        H2 = sb("A_hi_2", [P, TB, G * 32], F32R)
        y_in = sb("y_in", [P, 2, TB, D])
        sb("keep_x_hi", [P, 2, TB, D])
        L2 = sb("A_lo_2", [P, TB, G * 32], F32R)
        z_out = sb("z_out", [P, 2, TB, D])
        sb("keep_x_lo", [P, 2, TB, D])
        R2 = sb("A_rows_2", [P, 2, G, UC])

        R_slot = [R[:, 0], R[:, 1], R2[:, 0], R2[:, 1]]
        H_slot = [H[:, 0], H[:, 1], H2[:]]
        L_slot = [L[:, 0], L[:, 1], L2[:]]

        bank = [ctx.enter_context(nc.psum_tensor(f"bank{i}", [P, 512], F32)) for i in range(6)]
        acc, hidp, V, U = bank[0:2], bank[2:4], bank[4], bank[5]

        rows_in = [sem(f"rows_in{i}") for i in range(4)]
        x_in = [sem(f"x_in{v}") for v in range(UN)]
        weights_in = sem("weights_in")
        consts_in = sem("consts_in")
        xh_done, xl_done = sem("xh_done"), sem("xl_done")
        masks = sem("masks")
        scale_ready = sem("scale_ready")
        wt_done, wt_ready = sem("wt_done"), sem("wt_ready")
        t_done, deg_half = sem("t_done"), sem("deg_half")
        h_done = sem("h_done")
        pool_l, dve_l = sem("pool_l"), sem("dve_l")
        h_used, l_used, t_used = sem("h_used"), sem("l_used"), sem("t_used")
        acc1_done = sem("acc1_done")
        hid_ready, hid_done = sem("hid_ready"), sem("hid_done")
        deg_cols, deg_summed = sem("deg_cols"), sem("deg_summed")
        merged = sem("merged")
        norm_step, pow_done, y_done = sem("norm_step"), sem("pow_done"), sem("y_done")
        yt_done, yt_ready, support = sem("yt_done"), sem("yt_ready"), sem("support")
        s_step, sh_done, sl_done, yp_done = sem("s_step"), sem("sh_done"), sem("sl_done"), sem("yp_done")
        y_stored, plain_ready = sem("y_stored"), sem("plain_ready")
        prod_ready, prod_t = sem("prod_ready"), sem("prod_t")
        y_back = [sem(f"y_back{i}") for i in range(2)]
        norm2_step, pow2_done, out_ready = sem("norm2_step"), sem("pow2_done"), sem("out_ready")
        stored = [sem(f"stored{i}") for i in range(2)]
        NORM, SSTEP, NORM2 = 11, 2, 5

        x_stage_buf = [hid[:].rearrange("p t (s d) -> p (t s) d", d=D),
                       S32[:].rearrange("p t s d -> p (t s) d")]
        t3 = T[:, 3].rearrange("p t g i -> p (t g i)").rearrange("p (t s d) -> p t s d", t=2, d=D)
        stage = [x_stage_buf, [t3[:, 0], t3[:, 1]], x_stage_buf, x_stage_buf]
        w_stage = hid[:].rearrange("p t (s d) -> p (t s) d", d=D)
        w_last = S32[:, 0, 0, :]
        biases = S32[0:2 * LAYERS, 0, 1, :]

        def before(p, kinds):
            return sum(KINDS[i] in kinds for i in range(p))

        NSPLIT, NPOOL, NDVE, NPLAIN = (before(16, k) for k in ("PD", "P", "D", "F"))

        def split_no(r, p):
            return NSPLIT * r + before(p, "PD")

        def low_made(eng, r, p):
            if KINDS[p] == "P":
                eng.wait_ge(pool_l, TILES + NPOOL * r + before(p, "P") + 1)
            else:
                eng.wait_ge(dve_l, NDVE * r + before(p, "D") + 1)

        def slot_free(eng, r, p, used):
            s = before(p, "PD")
            if isinstance(r, int) and r == 0 and s < 3:
                if s < 2:
                    eng.wait_ge(used, TILES - 1 + s)
                else:
                    eng.wait_ge(l_used, TILES)
            else:
                eng.wait_ge(used, TILES + split_no(r, p) - 2)

        def low_was_made(eng, r, p):
            split = [i for i in range(16) if KINDS[i] != "F"]
            s = before(p, "PD")
            if s >= 3:
                low_made(eng, r, split[s - 3])
            elif not isinstance(r, int):
                low_made(eng, r - 1, split[s - 3])
            elif s < 2:
                eng.wait_ge(pool_l, TILES - 1 + s)

        block = ctx.enter_context(nc.Block())

        @block.sync
        def _(sp):
            def load_rows(slot, u, h, v):
                for a in range(4):
                    sp.dma_start(R_slot[slot][32 * a:32 * a + 32], A_v[u, h, v, a]).then_inc(rows_in[slot], 16)

            def load_x(v):
                for t in range(2):
                    for a in range(4):
                        sp.dma_start(stage[v][t][32 * a:32 * a + 32], x_stage[t][v, a]).then_inc(x_in[v], 16)

            def load_weights():
                for t, w in enumerate((W1, W2)):
                    sp.dma_start(w_stage[:, 3 * t:3 * t + 3, :], w.rearrange("l e d -> e l d")).then_inc(weights_in, 16)
                sp.dma_start(w_stage[:, 6:8, :], Wm.rearrange("e (s d) -> e s d", s=2)).then_inc(weights_in, 16)
                sp.dma_start(w_last, W).then_inc(weights_in, 16)
                for t, bias in enumerate((b1, b2)):
                    sp.dma_start(biases[LAYERS * t:LAYERS * t + LAYERS], bias).then_inc(weights_in, 16)

            load_x(0)
            load_rows(0, 0, 0, 0)
            load_x(1)
            sp.wait_ge(xl_done, 2)
            load_x(2)
            load_rows(1, 0, 0, 1)
            sp.wait_ge(deg_half, 2)
            load_rows(0, 0, 0, 2)
            sp.wait_ge(xl_done, 6)
            load_x(3)
            sp.wait_ge(deg_half, 4)
            load_rows(1, 0, 0, 3)
            sp.wait_ge(xl_done, 8)
            load_weights()

            def chunk_rows(c, u, h):
                for v in range(UN):
                    sp.wait_ge(deg_half, 8 * c + 2 * v - 2)
                    load_rows(v % 2, u, h, v)

            chunk_rows(1, 0, 1)
            with sp.Fori(1, UN) as u:
                for h in range(2):
                    chunk_rows(2 * u + h, u, h)

            def pair_rows(r):
                for n, (par, q) in enumerate(UNITS):
                    if isinstance(r, int) and n < 2:
                        sp.wait_ge(deg_half, TILES - 2 + 2 * n)
                    elif isinstance(r, int) and n < 4:
                        sp.wait_ge(l_used, TILES)
                    else:
                        sp.wait_ge(t_done, TILES + 16 * r + 2 * (n - 4) + 2)
                    load_rows(n % 4, r, par, q // 2)

            pair_rows(0)
            with sp.Fori(1, PAIRS) as r:
                pair_rows(r)

        @block.gpsimd
        def _(pool):
            nc.gpsimd.memset(ident[:], 0.0).then_inc(masks, 1)
            nc.gpsimd.memset(quad_sum[:], 0.0).then_inc(masks, 1)
            nc.gpsimd.memset(minus_half[:], -0.5).then_inc(masks, 1)
            pool.wait_ge(masks, 2)
            nc.gpsimd.affine_select(out=ident[:], in_=ident[:], compare_op=ALU.not_equal, fill=1.0, base=0,
                                    pattern=[[-1, P]], channel_multiplier=1).then_inc(masks, 1)
            for s in range(-3, 4):
                nc.gpsimd.affine_select(out=quad_sum[:], in_=quad_sum[:], compare_op=ALU.not_equal, fill=1.0,
                                        base=32 * s, pattern=[[-1, P]], channel_multiplier=1).then_inc(masks, 1)
                pool.wait_ge(masks, 8 + s)

            def low(dst, t, hi):
                return nc.gpsimd.tensor_tensor(dst.rearrange("p t n -> p (t n)"),
                                               t.rearrange("p t g i -> p (t g i)"),
                                               hi.rearrange("p t n -> p (t n)").bitcast(F32), ALU.subtract)

            def powers(pc):
                pool.wait_ge(norm_step, NORM * pc + 10)
                nc.gpsimd.tensor_tensor(rstd[:], var_eps[:], minus_half[:], ALU.pow).then_inc(pow_done, 1)
                nc.gpsimd.tensor_tensor(deg_pow[:], deg[:], minus_half[:], ALU.pow).then_inc(pow_done, 1)

            def chunk_low(c):
                start = isinstance(c, int) and c == 0
                for q in QS:
                    n = CH * c + q
                    pool.wait_ge(h_done, n + 1)
                    if not (start and q < 2):
                        pool.wait_ge(l_used, n - 1)
                    low(L[:, q % 2], T[:, q % 4], H[:, q % 2]).then_inc(pool_l, 1)
                    if q == 5 and not start:
                        powers(c - 1)

            chunk_low(0)
            with pool.Fori(1, CH) as c:
                chunk_low(c)

            def powers2(k):
                pool.wait_ge(norm2_step, NORM2 * k + NORM2)
                nc.gpsimd.tensor_tensor(rstd[:], var_eps[:], minus_half[:], ALU.pow).then_inc(pow2_done, 1)

            def pair_low(r):
                start = isinstance(r, int)
                for p, kind in enumerate(KINDS):
                    if kind == "P":
                        s = before(p, "PD") % 3
                        pool.wait_ge(h_done, TILES + split_no(r, p) + 1)
                        slot_free(pool, r, p, l_used)
                        low(L_slot[s], T[:, p % 4], H_slot[s]).then_inc(pool_l, 1)
                    if start and p == 6:
                        powers(CH - 1)
                    if not start and p == 4:
                        powers2(2 * r - 2)
                    if not start and p == 8:
                        powers2(2 * r - 1)

            pair_low(0)
            with pool.Fori(1, PAIRS) as r:
                pair_low(r)
            powers2(CH - 2)
            powers2(CH - 1)

        @block.scalar
        def _(act):
            nc_act = nc.scalar
            act.dma_start(bm_row[:], bm.rearrange("(o d) -> o d", o=1).to_broadcast([P, D])).then_inc(consts_in, 16)
            act.dma_start(b_row[:], b.rearrange("(o d) -> o d", o=1).to_broadcast([P, D])).then_inc(consts_in, 16)
            for t, e in enumerate((eps1, eps2)):
                act.dma_start(ax_scale[:, t:t + 1], e.rearrange("(o d) -> o d", o=1).to_broadcast([P, 1])).then_inc(consts_in, 16)

            def x_high(v):
                act.wait_ge(x_in[v], 128)
                for t in range(2):
                    dst = Xh[t][:, 2 * v:2 * v + 2].rearrange("p h b d -> p b h d")
                    nc_act.activation(dst, stage[v][t].rearrange("p (b h) d -> p b h d", h=2), ACT.Copy).then_inc(xh_done, 1)

            def high(dst, t):
                return nc_act.activation(dst.rearrange("p t n -> p (t n)"), t.rearrange("p t g i -> p (t g i)"), ACT.Copy)

            def take_ax(pc, t):
                if t == 0:
                    act.wait_ge(acc1_done, pc + 1)
                    if not (isinstance(pc, int) and pc == 0):
                        act.wait_ge(merged, pc)
                    else:
                        act.wait_ge(scale_ready, 1)
                        act.wait_ge(wt_done, 1)
                else:
                    act.wait_ge(l_used, CH * pc + CH)
                nc_act.activation(hid[:, t], acc[t][:], ACT.Copy, scale=ax_scale[:, t:t + 1]).then_inc(hid_ready, 1)

            def relu(pc, layer):
                for t in range(2):
                    act.wait_ge(hid_done, 2 * LAYERS * pc + 2 * layer + t + 1)
                    dst, src = hid[:, t], hidp[t][:]
                    if layer == LAYERS - 1:
                        dst = dst.rearrange("p (b a i) -> p a b i", a=4, b=TB)
                        src = src.rearrange("p (a b i) -> p a b i", a=4, b=TB)
                    i = LAYERS * t + layer
                    nc_act.activation(dst, src, ACT.Relu, bias=bT[:, i:i + 1]).then_inc(hid_ready, 1)

            def take_yt(pc, dst):
                act.wait_ge(yt_done, pc + 1)
                if not (isinstance(pc, int) and pc == 0):
                    act.wait_ge(support, pc)
                nc_act.activation(dst, U[:], ACT.Copy).then_inc(yt_ready, 1)

            def s_high(pc):
                act.wait_ge(s_step, SSTEP * pc + 2)
                nc_act.activation(Sh[:, pc], V[:].rearrange("p (b d) -> p b d", b=TB), ACT.Copy).then_inc(sh_done, 1)

            def store_y(pc, u, h, src):
                act.wait_ge(yp_done, pc + 1)
                for a in range(4):
                    act.dma_start(y_v[u, h, a], src[32 * a:32 * a + 32]).then_inc(y_stored, 16)

            def chunk_high(c, u=None, h=None):
                first = isinstance(c, int) and c == 0
                second = isinstance(c, int) and c == 1
                for q in QS:
                    n = CH * c + q
                    if first and q % 2 == 0:
                        x_high(q // 2)
                    act.wait_ge(t_done, n + 1)
                    if not (first and q < 2):
                        act.wait_ge(h_used, n - 1)
                        act.wait_ge(pool_l, n - 1)
                    high(H[:, q % 2], T[:, q % 4]).then_inc(h_done, 1)
                    if first:
                        if q == 7:
                            act.wait_ge(wt_done, 1)
                            nc_act.activation(WT[:, 0:4].rearrange("p s d -> p (s d)"), hidp[0][:], ACT.Copy).then_inc(wt_ready, 1)
                            nc_act.activation(WT[:, 4:8].rearrange("p s d -> p (s d)"), hidp[1][:], ACT.Copy).then_inc(wt_ready, 1)
                            nc_act.activation(WT[:, 8], V[:, 0:P], ACT.Copy).then_inc(wt_ready, 1)
                            nc_act.activation(bT[:], V[:, P:P + 2 * LAYERS], ACT.Copy).then_inc(wt_ready, 1)
                            act.wait_ge(wt_ready, 4)
                        continue
                    pc = c - 1
                    if q == 0:
                        take_ax(pc, 0)
                        take_ax(pc, 1)
                    if q == 1:
                        relu(pc, 0)
                    if q == 2:
                        relu(pc, 1)
                        if not second:
                            s_high(pc - 1)
                    if q == 3:
                        relu(pc, 2)
                    if q == 4 and not second:
                        store_y(pc - 1, u, h, S32[:, 0])
                    if q == 7:
                        take_yt(pc, S32[:, 1].rearrange("p b d -> p (b d)"))

            chunk_high(0)
            chunk_high(1)
            with act.Fori(1, UN) as u:
                for h in range(2):
                    chunk_high(2 * u + h, u - 1, h)

            def take_prod(r, par):
                k = 2 * r + par
                act.wait_ge(l_used, TILES + split_no(r, ORDER.index((par, CH - 1))) + 1)
                if isinstance(r, int) and r == 0:
                    act.wait_ge(support, CH)
                    act.wait_ge(y_stored, 64 * CH)
                elif par == 0:
                    act.wait_ge(prod_t, k - 1)
                else:
                    act.wait_ge(prod_t, k)
                nc_act.activation(hid[:, par].rearrange("p (b a i) -> p a b i", a=4, b=TB),
                                  acc[par][:].rearrange("p (a b i) -> p a b i", a=4, b=TB), ACT.Copy).then_inc(prod_ready, 1)

            def load_y(r, par):
                k = 2 * r + par
                if not (isinstance(r, int) and r == 0):
                    act.wait_ge(norm2_step, NORM2 * (k - 2) + 1)
                for a in range(4):
                    act.dma_start(y_in[32 * a:32 * a + 32, par], y_v[r, par, a]).then_inc(y_back[par], 16)

            def store_out(r, par):
                act.wait_ge(out_ready, 2 * r + par + 1)
                for a in range(4):
                    act.dma_start(out_v[r, par, a], z_out[32 * a:32 * a + 32, par]).then_inc(stored[par], 16)

            def pair_high(r):
                start = isinstance(r, int)
                for p, kind in enumerate(KINDS):
                    if kind != "F":
                        act.wait_ge(t_done, TILES + 16 * r + p + 1)
                        slot_free(act, r, p, h_used)
                        low_was_made(act, r, p)
                        high(H_slot[before(p, "PD") % 3], T[:, p % 4]).then_inc(h_done, 1)
                    if start:
                        if p == 0:
                            take_ax(CH - 1, 0)
                            take_ax(CH - 1, 1)
                            s_high(CH - 2)
                        if p == 1:
                            relu(CH - 1, 0)
                        if p == 2:
                            relu(CH - 1, 1)
                            store_y(CH - 2, UN - 1, 0, S32[:, 0])
                        if p == 3:
                            relu(CH - 1, 2)
                        if p == 9:
                            take_yt(CH - 1, hid[:, 0])
                        if p == 10:
                            s_high(CH - 1)
                            store_y(CH - 1, UN - 1, 1, hid[:, 1].rearrange("p (b d) -> p b d", b=TB))
                            act.wait_ge(y_stored, 64 * CH)
                            act.wait_ge(l_used, TILES)
                    else:
                        if p == 2:
                            take_prod(r - 1, 1)
                        if p == 8:
                            store_out(r - 1, 0)
                        if p == 10:
                            store_out(r - 1, 1)
                    if p == 13:
                        for par in range(2):
                            if not start:
                                act.wait_ge(stored[par], 64 * r)
                            load_y(r, par)
                take_prod(r, 0)

            pair_high(0)
            with act.Fori(1, PAIRS) as r:
                pair_high(r)
            take_prod(PAIRS - 1, 1)
            store_out(PAIRS - 1, 0)
            store_out(PAIRS - 1, 1)
            for par in range(2):
                act.wait_ge(stored[par], 64 * PAIRS)

        @block.vector
        def _(dve):
            def transpose_tile(slot, half, src):
                return nc.vector.transpose(T[:, slot], src.rearrange("p g (b h j) -> p h b g j", h=2, j=32)[:, half])

            def low(dst, t, hi):
                return nc.vector.tensor_tensor(dst.rearrange("p t n -> p (t n)"),
                                               t.rearrange("p t g i -> p (t g i)"),
                                               hi.rearrange("p t n -> p (t n)").bitcast(F32), ALU.subtract)

            def x_low(v):
                dve.wait_ge(xh_done, 2 * v + 2)
                for t in range(2):
                    hi = Xh[t][:, 2 * v:2 * v + 2].rearrange("p h b d -> p b h d").bitcast(F32)
                    lo = Xl[t][:, 2 * v:2 * v + 2].rearrange("p h b d -> p b h d")
                    nc.vector.tensor_tensor(lo, stage[v][t].rearrange("p (b h) d -> p b h d", h=2), hi,
                                            ALU.subtract).then_inc(xl_done, 1)

            def steps(signal, base):
                count = [0]

                def step(ins):
                    count[0] += 1
                    ins.then_inc(signal, 1)
                    dve.wait_ge(signal, base + count[0])
                return step

            def moments_of(z, step):
                for i in range(TB):
                    last = nc.vector.bn_stats(stats[:, i], z[:, i])
                step(last)
                even, odd = stats[:, :, 0:3], stats[:, :, 3:6]
                nc.vector.tensor_tensor(mean[:], even[:, :, 1], odd[:, :, 1], ALU.add)
                nc.vector.tensor_tensor(mean_diff[:], even[:, :, 1], odd[:, :, 1], ALU.subtract)
                step(nc.vector.tensor_tensor(var_eps[:], even[:, :, 2], odd[:, :, 2], ALU.add))
                nc.vector.tensor_scalar(mean[:], mean[:], 0.5, None, ALU.mult)
                nc.vector.tensor_tensor(mean_diff[:], mean_diff[:], mean_diff[:], ALU.mult)
                step(nc.vector.tensor_scalar(var_eps[:], var_eps[:], 1.0 / D, LN_EPS, ALU.mult, ALU.add))
                step(nc.vector.scalar_tensor_tensor(var_eps[:], mean_diff[:], 0.25, var_eps[:], ALU.mult, ALU.add))

            def norm1(pc, z):
                step = steps(norm_step, NORM * pc)
                dve.wait_ge(deg_summed, pc + 1)
                for a in range(4):
                    last = nc.vector.tensor_scalar(deg[32 * a:32 * a + 32], U[32 * a:32 * a + 32, 4 * a:4 * a + 4],
                                                   1.0, None, ALU.add)
                step(last)
                step(nc.vector.tensor_scalar(deg_zero[:], deg[:], 0.0, None, ALU.is_equal))
                step(nc.vector.tensor_tensor(deg[:], deg[:], deg_zero[:], ALU.add))
                dve.wait_ge(merged, pc + 1)
                if not (isinstance(pc, int) and pc == 0):
                    dve.wait_ge(y_stored, 64 * pc)
                step(nc.vector.tensor_tensor(z, V[:].rearrange("p (b d) -> p b d", b=TB),
                                             bm_row[:].unsqueeze(1).to_broadcast([P, TB, D]), ALU.add))
                step(nc.vector.tensor_tensor(z, z, Xh1[:, pc].bitcast(F32), ALU.add))
                step(nc.vector.tensor_tensor(z, z, Xl1[:, pc].bitcast(F32), ALU.add))
                moments_of(z, step)

            def norm1_end(pc, z):
                dve.wait_ge(pow_done, 2 * pc + 2)
                nc.vector.tensor_tensor(dinv[:], deg_pow[:], deg_zero[:], ALU.subtract).then_inc(norm_step, 1)
                for i in range(TB):
                    last = nc.vector.tensor_scalar(z[:, i], z[:, i], mean[:, i:i + 1], rstd[:, i:i + 1],
                                                   ALU.subtract, ALU.mult)
                last.then_inc(y_done, 1)
                dve.wait_ge(norm_step, NORM * pc + NORM)
                nc.vector.tensor_copy(dinv_all[:, pc], dinv[:])

            def support_end(pc, z):
                v4 = V[:].rearrange("p (b d) -> p b d", b=TB)
                step = steps(s_step, SSTEP * pc)
                dve.wait_ge(support, pc + 1)
                step(nc.vector.tensor_tensor(v4, v4, b_row[:].unsqueeze(1).to_broadcast([P, TB, D]), ALU.add))
                for i in range(TB):
                    last = nc.vector.tensor_scalar(v4[:, i], v4[:, i], dinv[:, i:i + 1], None, ALU.mult)
                step(last)
                dve.wait_ge(sh_done, pc + 1)
                nc.vector.tensor_tensor(Sl[:, pc], v4, Sh[:, pc].bitcast(F32), ALU.subtract).then_inc(sl_done, 1)
                dve.wait_ge(y_done, pc + 1)
                for i in range(TB):
                    last = nc.vector.scalar_tensor_tensor(z[:, i], v4[:, i], dinv[:, i:i + 1], z[:, i], ALU.mult, ALU.add)
                last.then_inc(yp_done, 1)

            def chunk_cols(c):
                first = isinstance(c, int) and c == 0
                second = isinstance(c, int) and c == 1
                for q in QS:
                    n, u = CH * c + q, q // 2
                    if first and q % 2 == 0:
                        x_low(u)
                    if first and q == 2:
                        dve.wait_ge(xl_done, 4)
                    if q % 2 == 0:
                        dve.wait_ge(rows_in[u % 2], 64 * (2 * c + u // 2 + 1))
                    if not (first and q < 4):
                        dve.wait_ge(pool_l, n - 3)
                    transpose_tile(q % 4, q % 2, R_slot[u % 2]).then_inc(t_done, 1)
                    if q == 0 and not first:
                        dve.wait_ge(deg_cols, c)
                    half = slice(8 * (q % 2), 8 * (q % 2) + 8)
                    nc.vector.tensor_reduce(deg_part[:, u, half], R_slot[u % 2][:, half], AX.X, ALU.add).then_inc(deg_half, 1)
                    if q == 2 and not (first or second):
                        support_end(c - 2, S32[:, 0])
                    if q == 6 and not first:
                        norm1(c - 1, S32[:, 0])
                    if q == 7:
                        if not first:
                            norm1_end(c - 1, S32[:, 0])
                            dve.wait_ge(deg_summed, c)
                        dve.wait_ge(deg_half, CH * c + CH)
                        nc.vector.tensor_reduce(deg_quad[:], deg_part[:].rearrange("p u g -> p g u"), AX.X,
                                                ALU.add).then_inc(deg_cols, 1)

            dve.wait_ge(consts_in, 64)
            nc.vector.tensor_scalar(ax_scale[:], ax_scale[:], 1.0, 1.0, ALU.add, ALU.add).then_inc(scale_ready, 1)
            chunk_cols(0)
            chunk_cols(1)
            with dve.Fori(2, CH) as c:
                chunk_cols(c)

            def plain(i):
                q = PLAIN[i]
                nc.vector.tensor_tensor(S32[:, 1 - i], Sh[:, q].bitcast(F32), Sl[:, q].bitcast(F32),
                                        ALU.add).then_inc(plain_ready, 1)

            def norm2(k, r, par):
                z = z_out[:, par]
                u4 = U[:].rearrange("p (b d) -> p b d", b=TB)
                step = steps(norm2_step, NORM2 * k)
                dve.wait_ge(prod_t, k + 1)
                dve.wait_ge(y_back[par], 64 * (r + 1))
                for i in range(TB):
                    last = nc.vector.scalar_tensor_tensor(z[:, i], u4[:, i], dinv_all[:, k, i:i + 1], y_in[:, par, i],
                                                          ALU.mult, ALU.add)
                step(last)
                moments_of(z, step)

            def norm2_end(k, par):
                z = z_out[:, par]
                dve.wait_ge(pow2_done, k + 1)
                for i in range(TB):
                    last = nc.vector.tensor_scalar(z[:, i], z[:, i], mean[:, i:i + 1], rstd[:, i:i + 1],
                                                   ALU.subtract, ALU.mult)
                last.then_inc(out_ready, 1)

            def pair_cols(r, prev):
                start = isinstance(r, int)
                for p in range(16):
                    n = p // 2
                    if p % 2 == 0:
                        loads = 16 if n % 4 < 2 else 0
                        dve.wait_ge(rows_in[n % 4], 64 * (loads + 2 * r + n // 4 + 1))
                    if start and p < 4:
                        dve.wait_ge(pool_l, TILES - 3 + p)
                    else:
                        rr, pp = (r, p - 4) if p >= 4 else (r - 1, p + 12)
                        if KINDS[pp] == "F":
                            dve.wait_ge(t_used, NPLAIN * rr + before(pp, "F") + 1)
                        else:
                            low_made(dve, rr, pp)
                    transpose_tile(p % 4, p % 2, R_slot[n % 4]).then_inc(t_done, 1)
                    if p > 0 and KINDS[p - 1] == "D":
                        s = before(p - 1, "PD") % 3
                        dve.wait_ge(h_done, TILES + split_no(r, p - 1) + 1)
                        slot_free(dve, r, p - 1, l_used)
                        low(L_slot[s], T[:, (p - 1) % 4], H_slot[s]).then_inc(dve_l, 1)
                    if start:
                        if p == 0:
                            support_end(CH - 2, S32[:, 0])
                            dve.wait_ge(support, CH - 1)
                            dve.wait_ge(sl_done, CH - 1)
                            plain(0)
                        if p == 3:
                            dve.wait_ge(y_stored, 64 * (CH - 1))
                            plain(1)
                        if p == 6:
                            norm1(CH - 1, z_last)
                        if p == 8:
                            norm1_end(CH - 1, z_last)
                        if p == 11:
                            support_end(CH - 1, z_last)
                    else:
                        if p == 3:
                            norm2(2 * r - 2, r - 1, 0)
                        if p == 5:
                            norm2_end(2 * r - 2, 0)
                        if p == 8:
                            norm2(2 * r - 1, r - 1, 1)
                        if p == 10:
                            norm2_end(2 * r - 1, 1)

            z_last = hid[:, 1].rearrange("p (b d) -> p b d", b=TB)
            pair_cols(0, None)
            with dve.Fori(1, PAIRS) as r:
                pair_cols(r, r - 1)
            for par in range(2):
                norm2(CH - 2 + par, PAIRS - 1, par)
                norm2_end(CH - 2 + par, par)

        @block.tensor
        def _(pe):
            mm = nc.tensor.matmul

            def transpose_weights():
                pe.wait_ge(weights_in, 96)
                pe.wait_ge(masks, 11)
                for i in range(8):
                    nc.tensor.transpose(hidp[i // 4][:, P * (i % 4):P * (i % 4) + P], w_stage[:, i], ident[:])
                nc.tensor.transpose(V[:, 0:P], w_last, ident[:])
                nc.tensor.transpose(V[:, P:P + 2 * LAYERS], biases, ident[0:2 * LAYERS, 0:2 * LAYERS]).then_inc(wt_done, 1)

            def layer(pc, i):
                if i == 0 and isinstance(pc, int) and pc == 0:
                    pe.wait_ge(wt_ready, 4)
                for t in range(2):
                    pe.wait_ge(hid_ready, 2 * (LAYERS + 1) * pc + 2 * i + t + 1)
                    mm(hidp[t][:], WT[:, LAYERS * t + i], hid[:, t], start=True, stop=True).then_inc(hid_done, 1)

            def degrees(pc):
                pe.wait_ge(deg_cols, pc + 1)
                if not (isinstance(pc, int) and pc == 0):
                    pe.wait_ge(yt_ready, pc)
                mm(U[:, 0:G], quad_sum[:], deg_quad[:], start=True, stop=True).then_inc(deg_summed, 1)

            def merge(pc):
                pe.wait_ge(hid_ready, 2 * (LAYERS + 1) * (pc + 1))
                if not (isinstance(pc, int) and pc == 0):
                    pe.wait_ge(yp_done, pc)
                for i in range(TB):
                    for t in range(2):
                        last = mm(V[:, P * i:P * i + P], hid[:, t, P * i:P * i + P], WT[:, 2 * LAYERS + t],
                                  start=t == 0, stop=t == 1)
                last.then_inc(merged, 1)

            def transpose_y(pc, z):
                pe.wait_ge(y_done, pc + 1)
                for i in range(TB):
                    last = nc.tensor.transpose(U[:, P * i:P * i + P], z[:, i], ident[:])
                last.then_inc(yt_done, 1)

            def supports(pc, yt):
                pe.wait_ge(yt_ready, pc + 1)
                for i in range(TB):
                    last = mm(V[:, P * i:P * i + P], yt[:, P * i:P * i + P], WT[:, 8], start=True, stop=True)
                last.then_inc(support, 1)

            yt = S32[:, 1].rearrange("p b d -> p (b d)")

            def chunk_product(c):
                first = isinstance(c, int) and c == 0
                for q in QS:
                    n = CH * c + q
                    if first and q % 2 == 0:
                        pe.wait_ge(xl_done, q + 2)
                    pe.wait_ge(h_done, n + 1)
                    for t in range(2):
                        if q == 0 and not first:
                            pe.wait_ge(hid_ready, 2 * (LAYERS + 1) * (c - 1) + t + 1)
                        for kk in range(TB):
                            mm(acc[t][:], Xh[t][:, q, kk], H[:, q % 2, kk], start=q == 0 and kk == 0, stop=False)
                            last = mm(acc[t][:], Xl[t][:, q, kk], H[:, q % 2, kk], start=False, stop=False)
                    last.then_inc(h_used, 1)
                    if first:
                        if q == 7:
                            transpose_weights()
                    else:
                        if q < LAYERS:
                            layer(c - 1, q)
                        if q == 2:
                            degrees(c - 1)
                        if q == 3:
                            merge(c - 1)
                        if q == 6:
                            transpose_y(c - 1, S32[:, 0])
                        if q == 7:
                            supports(c - 1, yt)
                    pe.wait_ge(pool_l, n + 1)
                    for t in range(2):
                        for kk in range(TB):
                            last = mm(acc[t][:], Xh[t][:, q, kk], L[:, q % 2, kk], start=False, stop=q == 7 and kk == TB - 1)
                        if q == 7 and t == 0:
                            last.then_inc(acc1_done, 1)
                    last.then_inc(l_used, 1)

            chunk_product(0)
            chunk_product(1)
            with pe.Fori(2, CH) as c:
                chunk_product(c)

            def transpose_product(k, par):
                pe.wait_ge(prod_ready, k + 1)
                if par == 1:
                    pe.wait_ge(norm2_step, NORM2 * (k - 1) + 1)
                for i in range(TB):
                    last = nc.tensor.transpose(U[:, P * i:P * i + P], hid[:, par, P * i:P * i + P], ident[:])
                last.then_inc(prod_t, 1)

            def pair_product(r):
                start = isinstance(r, int)
                for p, (par, q) in enumerate(ORDER):
                    if start and p == 0:
                        pe.wait_ge(sh_done, CH - 1)
                        pe.wait_ge(sl_done, CH - 1)
                    if start and p == 13:
                        pe.wait_ge(sh_done, CH)
                        pe.wait_ge(sl_done, CH)
                    if q == 0:
                        if start:
                            pe.wait_ge(hid_ready, 2 * (LAYERS + 1) * (CH - 1) + par + 1)
                        else:
                            pe.wait_ge(prod_ready, 2 * r - 1 + par)
                    first, end = q == 0, q == 7
                    a = acc[par][:]
                    if KINDS[p] == "F":
                        i = PLAIN.index(q)
                        pe.wait_ge(t_done, TILES + 16 * r + p + 1)
                        if start:
                            pe.wait_ge(plain_ready, i + 1)
                        for kk in range(TB):
                            last = mm(a, S32[:, 1 - i, kk], T[:, p % 4, kk].rearrange("p g i -> p (g i)"),
                                      start=False, stop=False)
                        last.then_inc(t_used, 1)
                    else:
                        s = before(p, "PD") % 3
                        pe.wait_ge(h_done, TILES + split_no(r, p) + 1)
                        for kk in range(TB):
                            mm(a, Sh[:, q, kk], H_slot[s][:, kk], start=first and kk == 0, stop=False)
                            last = mm(a, Sl[:, q, kk], H_slot[s][:, kk], start=False, stop=False)
                        last.then_inc(h_used, 1)
                    if start:
                        if p in (0, 1, 2):
                            layer(CH - 1, p)
                        if p == 2:
                            degrees(CH - 1)
                        if p == 4:
                            merge(CH - 1)
                        if p == 8:
                            transpose_y(CH - 1, hid[:, 1].rearrange("p (b d) -> p b d", b=TB))
                        if p == 9:
                            supports(CH - 1, hid[:, 0])
                    else:
                        if p == 0:
                            transpose_product(2 * r - 2, 0)
                        if p == 6:
                            transpose_product(2 * r - 1, 1)
                    if KINDS[p] != "F":
                        low_made(pe, r, p)
                        for kk in range(TB):
                            last = mm(a, Sh[:, q, kk], L_slot[s][:, kk], start=False, stop=end and kk == TB - 1)
                        last.then_inc(l_used, 1)

            pair_product(0)
            with pe.Fori(1, PAIRS) as r:
                pair_product(r)
            transpose_product(CH - 2, 0)
            transpose_product(CH - 1, 1)


_INS = ["x", "adj", "L0_gnn_x2", "L0_gnn_eps1", "L0_gnn_eps2", "L0_gnn_W1", "L0_gnn_b1", "L0_gnn_W2", "L0_gnn_b2",
        "L0_gnn_Wm", "L0_gnn_bm", "L1_gnn_W", "L1_gnn_b"]


def kernel(**inputs):
    import numpy as np
    import concourse.bacc as bacc
    from concourse.bass_utils import run_bass_kernel_spmd as run

    nc = bacc.Bacc("TRN2", target_bir_lowering=False, num_devices=1)
    arrays, args = {}, []
    for name in _INS:
        a = np.ascontiguousarray(inputs[name])
        arrays["in_" + name] = a
        args.append(nc.dram_tensor("in_" + name, a.shape, mybir.dt.from_np(a.dtype), kind="ExternalInput").ap())
    shape = inputs["x"].shape
    args.append(nc.dram_tensor("out_0", shape, F32, kind="ExternalOutput").ap())
    args.append(nc.dram_tensor("y_scratch", shape, F32, kind="Internal").ap())
    program(nc, *args)
    return run(nc, [arrays], core_ids=[0]).results[0]["out_0"]
```

```python
from contextlib import ExitStack

import concourse.bass as bass
from concourse import mybir

F32 = mybir.dt.float32
F32R = mybir.dt.float32r
ALU = mybir.AluOpType
ACT = mybir.ActivationFunctionType
AX = mybir.AxisListType

P = 128
LN_EPS = 1e-5
LAYERS = 3

ORDER = [(0, q) for q in range(6)] + [(1, q) for q in range(6)] + [(0, 6), (0, 7), (1, 6), (1, 7)]
PLAIN = [1, 4, 7]
SPLIT = [q not in PLAIN for _, q in ORDER]
UNITS = [ORDER[p] for p in range(0, len(ORDER), 2)]


def program(nc, x, adj, x2, eps1, eps2, W1, b1, W2, b2, Wm, bm, W, b, out, y_dram):
    N, D = x.shape
    G = 16
    CH = N // (32 * G)
    TB = 4
    UN = CH // 2
    UC = N // UN // 4
    QS = range(CH)
    PAIRS = CH // 2
    TILES = CH * CH
    assert D == P and UC == 256

    A_v = adj.rearrange("(u g h i) (v a k) -> u h v a i g k", u=UN, g=G, h=2, i=32, v=UN, a=4)
    x_stage = [t.rearrange("(v a t j) d -> v a j t d", v=UN, a=4, t=8, j=32) for t in (x, x2)]
    y_v = y_dram.rearrange("(u a b h j) d -> u h a j b d", u=UN, a=4, b=TB, h=2, j=32)
    out_v = out.rearrange("(u a b h j) d -> u h a j b d", u=UN, a=4, b=TB, h=2, j=32)

    with ExitStack() as ctx:
        def sb(name, shape, dt=F32, c=ctx):
            return c.enter_context(nc.sbuf_tensor(name, shape, dt))

        def sem(name):
            return ctx.enter_context(nc.semaphore(name))

        Sh = sb("S_hi", [P, CH, TB, D], F32R)
        Sl = sb("S_lo", [P, CH, TB, D], F32R)
        S32 = sb("S_plain", [P, 2, TB, D])
        hid = sb("hidden", [P, 2, TB * P])
        WT = sb("weights_T", [P, 9, P])
        ident_r = sb("ident", [P, P], F32R)
        quad_sum = sb("quad_sum", [P, P])
        bm_row = sb("bm_row", [P, D])
        b_row = sb("b_row", [P, D])
        bT = sb("bias_T", [P, 2 * LAYERS])
        ax_scale = sb("ax_scale", [P, 2])
        deg_part = sb("deg_part", [P, UN, G])
        deg_quad = sb("deg_quad", [P, G])
        deg = sb("deg", [P, TB])
        deg_zero = sb("deg_zero", [P, TB])
        deg_pow = sb("deg_pow", [P, TB])
        dinv = sb("dinv", [P, TB])
        dinv_all = sb("dinv_all", [P, CH, TB])
        stats = sb("stats", [P, TB, 6])
        mean = sb("mean", [P, TB])
        mean_diff = sb("mean_diff", [P, TB])
        var_eps = sb("var_eps", [P, TB])
        rstd = sb("rstd", [P, TB])
        minus_half = sb("minus_half", [P, TB])
        R = sb("A_rows", [P, 2, G, UC])
        T = sb("A_cols", [P, 4, TB, G, 32])
        H = sb("A_hi", [P, 2, TB, G * 32], F32R)
        L = sb("A_lo", [P, 2, TB, G * 32], F32R)
        with ExitStack() as first:
            Xh1 = sb("x_hi", [P, CH, TB, D], F32R, first)
            Xl1 = sb("x_lo", [P, CH, TB, D], F32R, first)
            Xh2 = sb("x2_hi", [P, CH, TB, D], F32R, first)
            Xl2 = sb("x2_lo", [P, CH, TB, D], F32R, first)
        Xh, Xl = (Xh1, Xh2), (Xl1, Xl2)
        H2 = sb("A_hi_2", [P, TB, G * 32], F32R)
        y_in = sb("y_in", [P, 2, TB, D])
        S32_late = sb("S_plain_late", [P, TB, D])
        sb("keep_x_hi", [P, TB, D])
        L2 = sb("A_lo_2", [P, TB, G * 32], F32R)
        z_out = sb("z_out", [P, 2, TB, D])
        sb("keep_x_lo", [P, 2, TB, D])
        R2 = sb("A_rows_2", [P, 2, G, UC])

        ident = ident_r[:].bitcast(F32)
        plain_S = dict(zip(PLAIN, (S32[:, 1], S32_late[:], S32[:, 0])))
        R_slot = [R[:, 0], R[:, 1], R2[:, 0], R2[:, 1]]
        H_slot = [H[:, 0], H[:, 1], H2[:]]
        L_slot = [L[:, 0], L[:, 1], L2[:]]

        bank = [ctx.enter_context(nc.psum_tensor(f"bank{i}", [P, 512], F32)) for i in range(6)]
        acc, hidp, V, U = bank[0:2], bank[2:4], bank[4], bank[5]

        rows_in = [sem(f"rows_in{i}") for i in range(4)]
        x_in = [[sem(f"x{t + 1}_in{v}") for v in range(UN)] for t in range(2)]
        weights_in = sem("weights_in")
        consts_in = sem("consts_in")
        xh_done, xl_done = sem("xh_done"), sem("xl_done")
        masks = sem("masks")
        scale_ready = sem("scale_ready")
        wt_done, wt_ready = sem("wt_done"), sem("wt_ready")
        t_done, deg_half = sem("t_done"), sem("deg_half")
        h_done = sem("h_done")
        l_done = sem("l_done")
        h_used, l_used, t_used = sem("h_used"), sem("l_used"), sem("t_used")
        acc1_done = sem("acc1_done")
        hid_ready, hid_done = sem("hid_ready"), sem("hid_done")
        deg_cols, deg_summed = sem("deg_cols"), sem("deg_summed")
        merged = sem("merged")
        norm_step, pow_done, y_done = sem("norm_step"), sem("pow_done"), sem("y_done")
        yt_done, yt_ready, support = sem("yt_done"), sem("yt_ready"), sem("support")
        s_step, sh_done, sl_done, yp_done = sem("s_step"), sem("sh_done"), sem("sl_done"), sem("yp_done")
        y_stored, plain_ready = sem("y_stored"), sem("plain_ready")
        prod_ready, prod_t = sem("prod_ready"), sem("prod_t")
        y_back = [sem(f"y_back{i}") for i in range(2)]
        norm2_step, pow2_done, out_ready = sem("norm2_step"), sem("pow2_done"), sem("out_ready")
        stored = [sem(f"stored{i}") for i in range(2)]
        NORM, SSTEP, NORM2 = 9, 2, 5

        x_stage_buf = [hid[:].rearrange("p t (s d) -> p (t s) d", d=D),
                       S32[:].rearrange("p t s d -> p (t s) d")]
        t3 = T[:, 3].rearrange("p t g i -> p (t g i)").rearrange("p (t s d) -> p t s d", t=2, d=D)
        stage = [x_stage_buf, [t3[:, 0], t3[:, 1]], x_stage_buf, x_stage_buf]
        w_stage = hid[:].rearrange("p t (s d) -> p (t s) d", d=D)
        w_last = S32[:, 0, 0, :]
        biases = S32[0:2 * LAYERS, 0, 1, :]

        def before(p, split=True):
            return sum(x == split for x in SPLIT[:p])

        NSPLIT, NPLAIN = before(16), before(16, False)
        SLOT_OF = [0, 1, 2, 0, 1, 2, 0, 1, 2, 1]
        assert len(SLOT_OF) == NSPLIT

        def slot_at(p):
            return SLOT_OF[before(p)]

        def split_no(r, p):
            return NSPLIT * r + before(p)

        def slot_free(eng, r, p, used):
            s = before(p)
            back = next(d for d in range(1, NSPLIT) if SLOT_OF[s - d] == SLOT_OF[s])
            if isinstance(r, int) and r == 0 and back > s:
                if SLOT_OF[s] < 2:
                    eng.wait_ge(used, TILES - 1 + SLOT_OF[s])
                else:
                    eng.wait_ge(l_used, TILES)
            else:
                eng.wait_ge(used, TILES + split_no(r, p) - back + 1)

        def tile_used(eng, r, p):
            if SPLIT[p]:
                eng.wait_ge(l_used, TILES + split_no(r, p) + 1)
            else:
                eng.wait_ge(t_used, NPLAIN * r + before(p, False) + 1)

        block = ctx.enter_context(nc.Block())

        @block.sync
        def _(sp):
            def load_rows(slot, u, h, v):
                for a in range(4):
                    sp.dma_start(R_slot[slot][32 * a:32 * a + 32], A_v[u, h, v, a]).then_inc(rows_in[slot], 16)

            def load_x(v, ts=(0, 1)):
                for t in ts:
                    for a in range(4):
                        sp.dma_start(stage[v][t][32 * a:32 * a + 32], x_stage[t][v, a]).then_inc(x_in[t][v], 16)

            def load_weights():
                for t, w in enumerate((W1, W2)):
                    sp.dma_start(w_stage[:, 3 * t:3 * t + 3, :], w.rearrange("l e d -> e l d")).then_inc(weights_in, 16)
                sp.dma_start(w_stage[:, 6:8, :], Wm.rearrange("e (s d) -> e s d", s=2)).then_inc(weights_in, 16)
                sp.dma_start(w_last, W).then_inc(weights_in, 16)
                for t, bias in enumerate((b1, b2)):
                    sp.dma_start(biases[LAYERS * t:LAYERS * t + LAYERS], bias).then_inc(weights_in, 16)

            load_x(0, [0])
            load_rows(0, 0, 0, 0)
            load_x(0, [1])
            load_x(1)
            load_rows(1, 0, 0, 1)
            sp.wait_ge(xl_done, 2)
            load_x(2)
            sp.wait_ge(deg_half, 2)
            load_rows(0, 0, 0, 2)
            sp.wait_ge(xl_done, 6)
            load_x(3)
            sp.wait_ge(deg_half, 4)
            load_rows(1, 0, 0, 3)
            sp.wait_ge(xl_done, 8)
            load_weights()

            def chunk_rows(c, u, h):
                for v in range(UN):
                    sp.wait_ge(deg_half, 8 * c + 2 * v - 2)
                    load_rows(v % 2, u, h, v)

            chunk_rows(1, 0, 1)
            with sp.Fori(1, UN) as u:
                for h in range(2):
                    chunk_rows(2 * u + h, u, h)

            def pair_rows(r):
                for n, (par, q) in enumerate(UNITS):
                    if isinstance(r, int) and n < 2:
                        sp.wait_ge(deg_half, TILES - 2 + 2 * n)
                    elif isinstance(r, int) and n < 4:
                        sp.wait_ge(l_used, TILES)
                    else:
                        sp.wait_ge(t_done, TILES + 16 * r + 2 * (n - 4) + 2)
                    load_rows(n % 4, r, par, q // 2)

            pair_rows(0)
            with sp.Fori(1, PAIRS) as r:
                pair_rows(r)

        @block.gpsimd
        def _(pool):
            nc.gpsimd.memset(ident, 0.0).then_inc(masks, 1)
            nc.gpsimd.memset(quad_sum[:], 0.0).then_inc(masks, 1)
            nc.gpsimd.memset(minus_half[:], -0.5).then_inc(masks, 1)
            pool.wait_ge(masks, 2)
            nc.gpsimd.affine_select(out=ident_r[:], in_=ident, compare_op=ALU.not_equal, fill=1.0, base=0,
                                    pattern=[[-1, P]], channel_multiplier=1).then_inc(masks, 1)
            for s in range(-3, 4):
                nc.gpsimd.affine_select(out=quad_sum[:], in_=quad_sum[:], compare_op=ALU.not_equal, fill=1.0,
                                        base=32 * s, pattern=[[-1, P]], channel_multiplier=1).then_inc(masks, 1)
                pool.wait_ge(masks, 8 + s)

            def low(dst, t, hi):
                return nc.gpsimd.tensor_tensor(dst.rearrange("p t n -> p (t n)"),
                                               t.rearrange("p t g i -> p (t g i)"),
                                               hi.rearrange("p t n -> p (t n)").bitcast(F32), ALU.subtract)

            def powers(pc):
                pool.wait_ge(norm_step, NORM * pc + NORM - 1)
                nc.gpsimd.tensor_tensor(rstd[:], var_eps[:], minus_half[:], ALU.pow).then_inc(pow_done, 1)
                nc.gpsimd.tensor_tensor(deg_pow[:], deg[:], minus_half[:], ALU.pow).then_inc(pow_done, 1)

            def chunk_low(c):
                start = isinstance(c, int) and c == 0
                for q in QS:
                    n = CH * c + q
                    pool.wait_ge(h_done, n + 1)
                    if not (start and q < 2):
                        pool.wait_ge(l_used, n - 1)
                    low(L[:, q % 2], T[:, q % 4], H[:, q % 2]).then_inc(l_done, 1)
                    if q == 5 and not start:
                        powers(c - 1)

            chunk_low(0)
            with pool.Fori(1, CH) as c:
                chunk_low(c)

            def powers2(k):
                pool.wait_ge(norm2_step, NORM2 * k + NORM2)
                nc.gpsimd.tensor_tensor(rstd[:], var_eps[:], minus_half[:], ALU.pow).then_inc(pow2_done, 1)

            def pair_low(r):
                start = isinstance(r, int)
                for p in range(16):
                    if SPLIT[p]:
                        s = slot_at(p)
                        pool.wait_ge(h_done, TILES + split_no(r, p) + 1)
                        slot_free(pool, r, p, l_used)
                        low(L_slot[s], T[:, p % 4], H_slot[s]).then_inc(l_done, 1)
                    if start and p == 6:
                        powers(CH - 1)
                    if not start and p == 0:
                        powers2(2 * r - 2)
                    if not start and p == 5:
                        powers2(2 * r - 1)

            pair_low(0)
            with pool.Fori(1, PAIRS) as r:
                pair_low(r)
            powers2(CH - 2)
            powers2(CH - 1)

        @block.scalar
        def _(act):
            nc_act = nc.scalar
            act.dma_start(bm_row[:], bm.rearrange("(o d) -> o d", o=1).to_broadcast([P, D])).then_inc(consts_in, 16)
            act.dma_start(b_row[:], b.rearrange("(o d) -> o d", o=1).to_broadcast([P, D])).then_inc(consts_in, 16)
            for t, e in enumerate((eps1, eps2)):
                act.dma_start(ax_scale[:, t:t + 1], e.rearrange("(o d) -> o d", o=1).to_broadcast([P, 1])).then_inc(consts_in, 16)

            def x_high(v, ts=(0, 1)):
                for t in ts:
                    act.wait_ge(x_in[t][v], 64)
                    dst = Xh[t][:, 2 * v:2 * v + 2].rearrange("p h b d -> p b h d")
                    nc_act.activation(dst, stage[v][t].rearrange("p (b h) d -> p b h d", h=2), ACT.Copy).then_inc(xh_done, 1)

            def high(dst, t):
                return nc_act.activation(dst.rearrange("p t n -> p (t n)"), t.rearrange("p t g i -> p (t g i)"), ACT.Copy)

            def take_ax(pc, t):
                if t == 0:
                    act.wait_ge(acc1_done, pc + 1)
                    if not (isinstance(pc, int) and pc == 0):
                        act.wait_ge(merged, pc)
                    else:
                        act.wait_ge(scale_ready, 1)
                        act.wait_ge(wt_done, 1)
                else:
                    act.wait_ge(l_used, CH * pc + CH)
                nc_act.activation(hid[:, t], acc[t][:], ACT.Copy, scale=ax_scale[:, t:t + 1]).then_inc(hid_ready, 1)

            def relu(pc, layer):
                for t in range(2):
                    act.wait_ge(hid_done, 2 * LAYERS * pc + 2 * layer + t + 1)
                    dst, src = hid[:, t], hidp[t][:]
                    if layer == LAYERS - 1:
                        dst = dst.rearrange("p (b a i) -> p a b i", a=4, b=TB)
                        src = src.rearrange("p (a b i) -> p a b i", a=4, b=TB)
                    i = LAYERS * t + layer
                    nc_act.activation(dst, src, ACT.Relu, bias=bT[:, i:i + 1]).then_inc(hid_ready, 1)

            def take_yt(pc, dst):
                act.wait_ge(yt_done, pc + 1)
                if not (isinstance(pc, int) and pc == 0):
                    act.wait_ge(support, pc)
                nc_act.activation(dst, U[:], ACT.Copy).then_inc(yt_ready, 1)

            def s_high(pc):
                act.wait_ge(s_step, SSTEP * pc + 2)
                nc_act.activation(Sh[:, pc], V[:].rearrange("p (b d) -> p b d", b=TB), ACT.Copy).then_inc(sh_done, 1)

            def store_y(pc, u, h, src):
                act.wait_ge(yp_done, pc + 1)
                for a in range(4):
                    act.dma_start(y_v[u, h, a], src[32 * a:32 * a + 32]).then_inc(y_stored, 16)

            def chunk_high(c, u=None, h=None):
                first = isinstance(c, int) and c == 0
                second = isinstance(c, int) and c == 1
                for q in QS:
                    n = CH * c + q
                    if first and q % 2 == 0:
                        x_high(q // 2, [0] if q == 0 else (0, 1))
                    act.wait_ge(t_done, n + 1)
                    if not (first and q < 2):
                        act.wait_ge(h_used, n - 1)
                        act.wait_ge(l_done, n - 1)
                    high(H[:, q % 2], T[:, q % 4]).then_inc(h_done, 1)
                    if first:
                        if q == 0:
                            x_high(0, [1])
                        if q == 7:
                            act.wait_ge(wt_done, 1)
                            nc_act.activation(WT[:, 0:4].rearrange("p s d -> p (s d)"), hidp[0][:], ACT.Copy).then_inc(wt_ready, 1)
                            nc_act.activation(WT[:, 4:8].rearrange("p s d -> p (s d)"), hidp[1][:], ACT.Copy).then_inc(wt_ready, 1)
                            nc_act.activation(WT[:, 8], V[:, 0:P], ACT.Copy).then_inc(wt_ready, 1)
                            nc_act.activation(bT[:], V[:, P:P + 2 * LAYERS], ACT.Copy).then_inc(wt_ready, 1)
                            act.wait_ge(wt_ready, 4)
                        continue
                    pc = c - 1
                    if q == 0:
                        take_ax(pc, 0)
                        take_ax(pc, 1)
                    if q == 1:
                        if not second:
                            s_high(pc - 1)
                        relu(pc, 0)
                    if q == 2:
                        relu(pc, 1)
                    if q == 3:
                        relu(pc, 2)
                    if q == 4 and not second:
                        store_y(pc - 1, u, h, S32[:, 0])
                    if q == 7:
                        take_yt(pc, S32[:, 1].rearrange("p b d -> p (b d)"))

            chunk_high(0)
            chunk_high(1)
            with act.Fori(1, UN) as u:
                for h in range(2):
                    chunk_high(2 * u + h, u - 1, h)

            def take_prod(r, par):
                k = 2 * r + par
                tile_used(act, r, ORDER.index((par, CH - 1)))
                if isinstance(r, int) and r == 0:
                    act.wait_ge(support, CH)
                elif par == 0:
                    act.wait_ge(prod_t, k - 1)
                else:
                    act.wait_ge(prod_t, k)
                nc_act.activation(hid[:, par].rearrange("p (b a i) -> p a b i", a=4, b=TB),
                                  acc[par][:].rearrange("p (a b i) -> p a b i", a=4, b=TB), ACT.Copy).then_inc(prod_ready, 1)

            def load_y(r, par):
                k = 2 * r + par
                if not (isinstance(r, int) and r == 0):
                    act.wait_ge(norm2_step, NORM2 * (k - 2) + 1)
                act.wait_ge(y_stored, 64 * k + 64)
                for a in range(4):
                    act.dma_start(y_in[32 * a:32 * a + 32, par], y_v[r, par, a]).then_inc(y_back[par], 16)

            def store_out(r, par):
                act.wait_ge(out_ready, 2 * r + par + 1)
                for a in range(4):
                    act.dma_start(out_v[r, par, a], z_out[32 * a:32 * a + 32, par]).then_inc(stored[par], 16)

            def pair_high(r):
                start = isinstance(r, int)
                for p in range(16):
                    if SPLIT[p]:
                        act.wait_ge(t_done, TILES + 16 * r + p + 1)
                        slot_free(act, r, p, h_used)
                        slot_free(act, r, p, l_done)
                        high(H_slot[slot_at(p)], T[:, p % 4]).then_inc(h_done, 1)
                    if start:
                        if p == 0:
                            take_ax(CH - 1, 0)
                            take_ax(CH - 1, 1)
                        if p == 2:
                            s_high(CH - 2)
                            relu(CH - 1, 0)
                        if p == 3:
                            relu(CH - 1, 1)
                            store_y(CH - 2, UN - 1, 0, S32[:, 0])
                        if p == 5:
                            relu(CH - 1, 2)
                        if p == 9:
                            take_yt(CH - 1, hid[:, 0])
                        if p == 11:
                            s_high(CH - 1)
                        if p == 14:
                            store_y(CH - 1, UN - 1, 1, hid[:, 1].rearrange("p (b d) -> p b d", b=TB))
                    else:
                        if p == 0:
                            take_prod(r - 1, 1)
                        if p == 5:
                            store_out(r - 1, 0)
                        if p == 9:
                            store_out(r - 1, 1)
                    if p == 13:
                        if start:
                            act.wait_ge(l_used, TILES)
                        for par in range(2):
                            if not start:
                                act.wait_ge(stored[par], 64 * r)
                            load_y(r, par)
                take_prod(r, 0)
                if start:
                    act.wait_ge(y_stored, 64 * CH)

            pair_high(0)
            with act.Fori(1, PAIRS) as r:
                pair_high(r)
            take_prod(PAIRS - 1, 1)
            store_out(PAIRS - 1, 0)
            store_out(PAIRS - 1, 1)
            for par in range(2):
                act.wait_ge(stored[par], 64 * PAIRS)

        @block.vector
        def _(dve):
            def transpose_tile(slot, half, src):
                return nc.vector.transpose(T[:, slot], src.rearrange("p g (b h j) -> p h b g j", h=2, j=32)[:, half])

            def x_low(v, ts=(0, 1)):
                for t in ts:
                    dve.wait_ge(xh_done, 2 * v + t + 1)
                    hi = Xh[t][:, 2 * v:2 * v + 2].rearrange("p h b d -> p b h d").bitcast(F32)
                    lo = Xl[t][:, 2 * v:2 * v + 2].rearrange("p h b d -> p b h d")
                    nc.vector.tensor_tensor(lo, stage[v][t].rearrange("p (b h) d -> p b h d", h=2), hi,
                                            ALU.subtract).then_inc(xl_done, 1)

            def steps(signal, base):
                count = [0]

                def step(ins):
                    count[0] += 1
                    ins.then_inc(signal, 1)
                    dve.wait_ge(signal, base + count[0])
                return step

            def moments_of(z, step):
                for i in range(TB):
                    last = nc.vector.bn_stats(stats[:, i], z[:, i])
                step(last)
                even, odd = stats[:, :, 0:3], stats[:, :, 3:6]
                nc.vector.tensor_tensor(mean[:], even[:, :, 1], odd[:, :, 1], ALU.add)
                nc.vector.tensor_tensor(mean_diff[:], even[:, :, 1], odd[:, :, 1], ALU.subtract)
                step(nc.vector.tensor_tensor(var_eps[:], even[:, :, 2], odd[:, :, 2], ALU.add))
                nc.vector.tensor_scalar(mean[:], mean[:], 0.5, None, ALU.mult)
                nc.vector.tensor_tensor(mean_diff[:], mean_diff[:], mean_diff[:], ALU.mult)
                step(nc.vector.tensor_scalar(var_eps[:], var_eps[:], 1.0 / D, LN_EPS, ALU.mult, ALU.add))
                step(nc.vector.scalar_tensor_tensor(var_eps[:], mean_diff[:], 0.25, var_eps[:], ALU.mult, ALU.add))

            def norm1(pc, z):
                step = steps(norm_step, NORM * pc)
                dve.wait_ge(deg_summed, pc + 1)
                for a in range(4):
                    last = nc.vector.tensor_scalar(deg[32 * a:32 * a + 32], U[32 * a:32 * a + 32, 4 * a:4 * a + 4],
                                                   1.0, None, ALU.add)
                step(last)
                step(nc.vector.tensor_scalar(deg_zero[:], deg[:], 0.0, None, ALU.is_equal))
                step(nc.vector.tensor_tensor(deg[:], deg[:], deg_zero[:], ALU.add))
                dve.wait_ge(merged, pc + 1)
                if not (isinstance(pc, int) and pc == 0):
                    dve.wait_ge(y_stored, 64 * pc)
                step(nc.vector.tensor_tensor(z, V[:].rearrange("p (b d) -> p b d", b=TB),
                                             bm_row[:].unsqueeze(1).to_broadcast([P, TB, D]), ALU.add))
                moments_of(z, step)

            def norm1_end(pc, z):
                dve.wait_ge(pow_done, 2 * pc + 2)
                nc.vector.tensor_tensor(dinv[:], deg_pow[:], deg_zero[:], ALU.subtract).then_inc(norm_step, 1)
                for i in range(TB):
                    last = nc.vector.tensor_scalar(z[:, i], z[:, i], mean[:, i:i + 1], rstd[:, i:i + 1],
                                                   ALU.subtract, ALU.mult)
                last.then_inc(y_done, 1)
                dve.wait_ge(norm_step, NORM * pc + NORM)
                nc.vector.tensor_copy(dinv_all[:, pc], dinv[:])

            v4 = V[:].rearrange("p (b d) -> p b d", b=TB)

            def support_scale(pc):
                step = steps(s_step, SSTEP * pc)
                dve.wait_ge(support, pc + 1)
                step(nc.vector.tensor_tensor(v4, v4, b_row[:].unsqueeze(1).to_broadcast([P, TB, D]), ALU.add))
                for i in range(TB):
                    last = nc.vector.tensor_scalar(v4[:, i], v4[:, i], dinv[:, i:i + 1], None, ALU.mult)
                last.then_inc(s_step, 1)

            def support_end(pc, z):
                dve.wait_ge(sh_done, pc + 1)
                nc.vector.tensor_tensor(Sl[:, pc], v4, Sh[:, pc].bitcast(F32), ALU.subtract).then_inc(sl_done, 1)
                dve.wait_ge(y_done, pc + 1)
                for i in range(TB):
                    last = nc.vector.scalar_tensor_tensor(z[:, i], v4[:, i], dinv[:, i:i + 1], z[:, i], ALU.mult, ALU.add)
                last.then_inc(yp_done, 1)

            def chunk_cols(c):
                first = isinstance(c, int) and c == 0
                second = isinstance(c, int) and c == 1
                for q in QS:
                    n, u = CH * c + q, q // 2
                    if first and q % 2 == 0:
                        x_low(u, [0] if q == 0 else (0, 1))
                    if first and q == 2:
                        dve.wait_ge(xl_done, 4)
                    if q % 2 == 0:
                        dve.wait_ge(rows_in[u % 2], 64 * (2 * c + u // 2 + 1))
                    if not (first and q < 4):
                        dve.wait_ge(l_done, n - 3)
                    transpose_tile(q % 4, q % 2, R_slot[u % 2]).then_inc(t_done, 1)
                    if q == 0 and first:
                        x_low(0, [1])
                    if q == 0 and not first:
                        dve.wait_ge(deg_cols, c)
                    half = slice(8 * (q % 2), 8 * (q % 2) + 8)
                    nc.vector.tensor_reduce(deg_part[:, u, half], R_slot[u % 2][:, half], AX.X, ALU.add).then_inc(deg_half, 1)
                    if q == 1 and not (first or second):
                        support_scale(c - 2)
                    if q == 2 and not (first or second):
                        support_end(c - 2, S32[:, 0])
                    if q == 5 and not first:
                        norm1(c - 1, S32[:, 0])
                    if q == 6 and not first:
                        norm1_end(c - 1, S32[:, 0])
                    if q == 7:
                        if not first:
                            dve.wait_ge(deg_summed, c)
                        dve.wait_ge(deg_half, CH * c + CH)
                        nc.vector.tensor_reduce(deg_quad[:], deg_part[:].rearrange("p u g -> p g u"), AX.X,
                                                ALU.add).then_inc(deg_cols, 1)

            dve.wait_ge(consts_in, 64)
            nc.vector.tensor_scalar(ax_scale[:], ax_scale[:], 1.0, 1.0, ALU.add, ALU.add).then_inc(scale_ready, 1)
            chunk_cols(0)
            chunk_cols(1)
            with dve.Fori(2, CH) as c:
                chunk_cols(c)

            def plain(i):
                q = PLAIN[i]
                nc.vector.tensor_tensor(plain_S[q], Sh[:, q].bitcast(F32), Sl[:, q].bitcast(F32),
                                        ALU.add).then_inc(plain_ready, 1)

            def norm2(k, r, par):
                z = z_out[:, par]
                u4 = U[:].rearrange("p (b d) -> p b d", b=TB)
                step = steps(norm2_step, NORM2 * k)
                dve.wait_ge(prod_t, k + 1)
                dve.wait_ge(y_back[par], 64 * (r + 1))
                for i in range(TB):
                    last = nc.vector.scalar_tensor_tensor(z[:, i], u4[:, i], dinv_all[:, k, i:i + 1], y_in[:, par, i],
                                                          ALU.mult, ALU.add)
                step(last)
                moments_of(z, step)

            def norm2_end(k, par):
                z = z_out[:, par]
                dve.wait_ge(pow2_done, k + 1)
                for i in range(TB):
                    last = nc.vector.tensor_scalar(z[:, i], z[:, i], mean[:, i:i + 1], rstd[:, i:i + 1],
                                                   ALU.subtract, ALU.mult)
                last.then_inc(out_ready, 1)

            def pair_cols(r, prev):
                start = isinstance(r, int)
                for p in range(16):
                    n = p // 2
                    if p % 2 == 0:
                        loads = 16 if n % 4 < 2 else 0
                        dve.wait_ge(rows_in[n % 4], 64 * (loads + 2 * r + n // 4 + 1))
                    if start and p < 4:
                        dve.wait_ge(l_done, TILES - 3 + p)
                    else:
                        rr, pp = (r, p - 4) if p >= 4 else (r - 1, p + 12)
                        if SPLIT[pp]:
                            dve.wait_ge(l_done, TILES + split_no(rr, pp) + 1)
                        else:
                            tile_used(dve, rr, pp)
                    transpose_tile(p % 4, p % 2, R_slot[n % 4]).then_inc(t_done, 1)
                    if start:
                        if p == 2:
                            support_scale(CH - 2)
                            plain(0)
                        if p == 3:
                            support_end(CH - 2, S32[:, 0])
                            dve.wait_ge(l_used, TILES)
                            plain(1)
                        if p == 6:
                            norm1(CH - 1, z_last)
                        if p == 8:
                            norm1_end(CH - 1, z_last)
                        if p == 11:
                            support_scale(CH - 1)
                        if p == 12:
                            support_end(CH - 1, z_last)
                            dve.wait_ge(sl_done, CH)
                            dve.wait_ge(y_stored, 64 * (CH - 1))
                            plain(2)
                    else:
                        if p == 1:
                            norm2(2 * r - 2, r - 1, 0)
                        if p == 3:
                            norm2_end(2 * r - 2, 0)
                        if p == 5:
                            norm2(2 * r - 1, r - 1, 1)
                        if p == 8:
                            norm2_end(2 * r - 1, 1)

            z_last = hid[:, 1].rearrange("p (b d) -> p b d", b=TB)
            pair_cols(0, None)
            with dve.Fori(1, PAIRS) as r:
                pair_cols(r, r - 1)
            for par in range(2):
                norm2(CH - 2 + par, PAIRS - 1, par)
                norm2_end(CH - 2 + par, par)

        @block.tensor
        def _(pe):
            mm = nc.tensor.matmul

            def transpose_weights():
                pe.wait_ge(weights_in, 96)
                pe.wait_ge(masks, 11)
                for i in range(8):
                    nc.tensor.transpose(hidp[i // 4][:, P * (i % 4):P * (i % 4) + P], w_stage[:, i], ident)
                nc.tensor.transpose(V[:, 0:P], w_last, ident)
                nc.tensor.transpose(V[:, P:P + 2 * LAYERS], biases, ident_r[0:2 * LAYERS, 0:2 * LAYERS].bitcast(F32)).then_inc(wt_done, 1)

            def layer(pc, i):
                if i == 0 and isinstance(pc, int) and pc == 0:
                    pe.wait_ge(wt_ready, 4)
                for t in range(2):
                    pe.wait_ge(hid_ready, 2 * (LAYERS + 1) * pc + 2 * i + t + 1)
                    mm(hidp[t][:], WT[:, LAYERS * t + i], hid[:, t], start=True, stop=True).then_inc(hid_done, 1)

            def degrees(pc):
                pe.wait_ge(deg_cols, pc + 1)
                if not (isinstance(pc, int) and pc == 0):
                    pe.wait_ge(yt_ready, pc)
                mm(U[:, 0:G], quad_sum[:], deg_quad[:], start=True, stop=True).then_inc(deg_summed, 1)

            def merge(pc):
                pe.wait_ge(hid_ready, 2 * (LAYERS + 1) * (pc + 1))
                if not (isinstance(pc, int) and pc == 0):
                    pe.wait_ge(yp_done, pc)
                mm(V[:], ident_r[:], Xh1[:, pc].rearrange("p b d -> p (b d)"), start=True, stop=False)
                mm(V[:], ident_r[:], Xl1[:, pc].rearrange("p b d -> p (b d)"), start=False, stop=False)
                for i in range(TB):
                    for t in range(2):
                        last = mm(V[:, P * i:P * i + P], hid[:, t, P * i:P * i + P], WT[:, 2 * LAYERS + t],
                                  start=False, stop=(i, t) == (TB - 1, 1))
                last.then_inc(merged, 1)

            def transpose_y(pc, z):
                pe.wait_ge(y_done, pc + 1)
                for i in range(TB):
                    last = nc.tensor.transpose(U[:, P * i:P * i + P], z[:, i], ident)
                last.then_inc(yt_done, 1)

            def supports(pc, yt):
                pe.wait_ge(yt_ready, pc + 1)
                for i in range(TB):
                    last = mm(V[:, P * i:P * i + P], yt[:, P * i:P * i + P], WT[:, 8], start=True, stop=True)
                last.then_inc(support, 1)

            yt = S32[:, 1].rearrange("p b d -> p (b d)")

            def chunk_product(c):
                first = isinstance(c, int) and c == 0
                for q in QS:
                    n = CH * c + q
                    if first and q % 2 == 0:
                        pe.wait_ge(xl_done, 1 if q == 0 else q + 2)
                    pe.wait_ge(h_done, n + 1)
                    for t in range(2):
                        if first and q == 0 and t == 1:
                            pe.wait_ge(xl_done, 2)
                        if q == 0 and not first:
                            pe.wait_ge(hid_ready, 2 * (LAYERS + 1) * (c - 1) + t + 1)
                        for kk in range(TB):
                            mm(acc[t][:], Xh[t][:, q, kk], H[:, q % 2, kk], start=q == 0 and kk == 0, stop=False)
                            last = mm(acc[t][:], Xl[t][:, q, kk], H[:, q % 2, kk], start=False, stop=False)
                    last.then_inc(h_used, 1)
                    if first:
                        if q == 7:
                            transpose_weights()
                    else:
                        if q < LAYERS:
                            layer(c - 1, q)
                        if q == 2:
                            degrees(c - 1)
                        if q == 3:
                            merge(c - 1)
                        if q == 6:
                            transpose_y(c - 1, S32[:, 0])
                        if q == 7:
                            supports(c - 1, yt)
                    pe.wait_ge(l_done, n + 1)
                    for t in range(2):
                        for kk in range(TB):
                            last = mm(acc[t][:], Xh[t][:, q, kk], L[:, q % 2, kk], start=False, stop=q == 7 and kk == TB - 1)
                        if q == 7 and t == 0:
                            last.then_inc(acc1_done, 1)
                    last.then_inc(l_used, 1)

            chunk_product(0)
            chunk_product(1)
            with pe.Fori(2, CH) as c:
                chunk_product(c)

            def transpose_product(k, par):
                pe.wait_ge(prod_ready, k + 1)
                if isinstance(k, int) and k == 0:
                    pe.wait_ge(yt_ready, CH)
                else:
                    pe.wait_ge(norm2_step, NORM2 * (k - 1) + 1)
                for i in range(TB):
                    last = nc.tensor.transpose(U[:, P * i:P * i + P], hid[:, par, P * i:P * i + P], ident)
                last.then_inc(prod_t, 1)

            def pair_product(r):
                start = isinstance(r, int)
                for p, (par, q) in enumerate(ORDER):
                    if start and q in (0, CH - 2):
                        pe.wait_ge(sh_done, CH - 2 if q == 0 else CH - 1)
                        pe.wait_ge(sl_done, CH - 2 if q == 0 else CH - 1)
                    if q == 0:
                        if start:
                            pe.wait_ge(hid_ready, 2 * (LAYERS + 1) * (CH - 1) + par + 1)
                        else:
                            pe.wait_ge(prod_ready, 2 * r - 1 + par)
                    first, end = q == 0, q == 7
                    a = acc[par][:]
                    if SPLIT[p]:
                        slot = slot_at(p)
                        pe.wait_ge(h_done, TILES + split_no(r, p) + 1)
                        for kk in range(TB):
                            mm(a, Sh[:, q, kk], H_slot[slot][:, kk], start=first and kk == 0, stop=False)
                            last = mm(a, Sl[:, q, kk], H_slot[slot][:, kk], start=False, stop=False)
                        last.then_inc(h_used, 1)
                    else:
                        pe.wait_ge(t_done, TILES + 16 * r + p + 1)
                        if start:
                            pe.wait_ge(plain_ready, PLAIN.index(q) + 1)
                        for kk in range(TB):
                            last = mm(a, plain_S[q][:, kk], T[:, p % 4, kk].rearrange("p g i -> p (g i)"),
                                      start=False, stop=end and kk == TB - 1)
                        last.then_inc(t_used, 1)
                    if start:
                        if p in (0, 1, 2):
                            layer(CH - 1, p)
                        if p == 2:
                            degrees(CH - 1)
                        if p == 4:
                            merge(CH - 1)
                        if p == 8:
                            transpose_y(CH - 1, hid[:, 1].rearrange("p (b d) -> p b d", b=TB))
                        if p == 9:
                            supports(CH - 1, hid[:, 0])
                    elif p == 2:
                        transpose_product(2 * r - 1, 1)
                    if p == 14:
                        transpose_product(2 * r, 0)
                    if SPLIT[p]:
                        pe.wait_ge(l_done, TILES + split_no(r, p) + 1)
                        for kk in range(TB):
                            last = mm(a, Sh[:, q, kk], L_slot[slot][:, kk], start=False, stop=False)
                        last.then_inc(l_used, 1)

            pair_product(0)
            with pe.Fori(1, PAIRS) as r:
                pair_product(r)
            transpose_product(CH - 1, 1)


_INS = ["x", "adj", "L0_gnn_x2", "L0_gnn_eps1", "L0_gnn_eps2", "L0_gnn_W1", "L0_gnn_b1", "L0_gnn_W2", "L0_gnn_b2",
        "L0_gnn_Wm", "L0_gnn_bm", "L1_gnn_W", "L1_gnn_b"]


def kernel(**inputs):
    import numpy as np
    import concourse.bacc as bacc
    from concourse.bass_utils import run_bass_kernel_spmd as run

    nc = bacc.Bacc("TRN2", target_bir_lowering=False, num_devices=1)
    arrays, args = {}, []
    for name in _INS:
        a = np.ascontiguousarray(inputs[name])
        arrays["in_" + name] = a
        args.append(nc.dram_tensor("in_" + name, a.shape, mybir.dt.from_np(a.dtype), kind="ExternalInput").ap())
    shape = inputs["x"].shape
    args.append(nc.dram_tensor("out_0", shape, F32, kind="ExternalOutput").ap())
    args.append(nc.dram_tensor("y_scratch", shape, F32, kind="Internal").ap())
    program(nc, *args)
    return run(nc, [arrays], core_ids=[0]).results[0]["out_0"]
```

```python
from contextlib import ExitStack

import concourse.bass as bass
from concourse import mybir

F32 = mybir.dt.float32
F32R = mybir.dt.float32r
ALU = mybir.AluOpType
ACT = mybir.ActivationFunctionType
AX = mybir.AxisListType

P = 128
LN_EPS = 1e-5
LAYERS = 3
CHUNKS = 8
LAG = 2


def groups1(c):
    return [2 * ((c // 2 + i // 2) % (CHUNKS // 2)) + i % 2 for i in range(CHUNKS)]


TILES1, UNITS1 = [], []
for c in range(CHUNKS):
    for i, q in enumerate(groups1(c)):
        TILES1.append((c, i, c, q))
        if i % 2 == 1:
            UNITS1.append((c, q // 2, len(TILES1) - 1))
        if i == 5 and c % 2 == 1 and c > LAG:
            TILES1.append((c, None, c - 1, c - LAG))
            UNITS1.append((c - 1, (c - LAG) // 2, len(TILES1) - 1))
TILES = len(TILES1)
END1 = [1 + max(n for n in range(TILES) if TILES1[n][0] == c) for c in range(CHUNKS)]
UNIT_OF1 = [min(U for U in range(len(UNITS1)) if n <= UNITS1[U][2]) for n in range(TILES)]


def groups2(c):
    return range(c // 2 * 2, CHUNKS)


ORDER = [0, 1, 2, 7, 4, 6, 5, 3]
TILES2 = ([(c, q) for c in (0, 1) for q in range(6)] + [(2, 2), (2, 3)] + [(c, q) for c in (0, 1) for q in (6, 7)]
          + [(2, q) for q in range(4, 8)] + [(c, q) for c in ORDER[3:] for q in groups2(c)])
M = len(TILES2)
FIRST = [min(m for m in range(M) if TILES2[m][0] == c) for c in ORDER]
LAST = [max(m for m in range(M) if TILES2[m][0] == c) for c in ORDER]
UNITS2 = []
UNIT_OF = []
for c, q in TILES2:
    if not UNITS2 or UNITS2[-1] != (c, q // 2):
        UNITS2.append((c, q // 2))
    UNIT_OF.append(len(UNITS2) - 1)
LAST_OF_UNIT = [max(m for m in range(M) if UNIT_OF[m] == n) for n in range(len(UNITS2))]
PLAIN = [2, 4, 7]
SPLIT = [q not in PLAIN for _, q in TILES2]
FIRST_OF_GROUP = {q: min(m for m in range(M) if TILES2[m][1] == q) for q in range(CHUNKS)}
TAKE_AT = [LAST[j] + 2 for j in range(CHUNKS)]
NORM_AT, TRANSPOSE_AT = [], []
for j in range(CHUNKS):
    TRANSPOSE_AT.append(max(TAKE_AT[j], NORM_AT[-1] - 2 if j else 0))
    NORM_AT.append(max(LAST[j] + 7, NORM_AT[-1] + 3 if j else 0))
NORM_END_AT = [m + 3 for m in NORM_AT]
STORE_AT = [m + 1 for m in NORM_END_AT]
POSTS_END = STORE_AT[-1] + 1
LOAD_Y_AT = [6, 8, 14, 17] + [STORE_AT[j] + 2 for j in range(CHUNKS - 4)]
T_RING = 6
T_OF = [(m if m < T_RING - 1 else m + 1) % T_RING for m in range(M)]
STAY = CHUNKS - 2
BACK = [j for j in range(CHUNKS) if LAG <= ORDER[j] < STAY]
LOAD_PART_AT = [2, 8, 9] + [FIRST[BACK[i]] + 2 for i in range(len(BACK) - 3)]
BANK2 = [0, 1, 4, 3, 0, 2, 1, 4]
BEFORE = [max([i for i in range(j) if BANK2[i] == BANK2[j]], default=None) for j in range(CHUNKS)]
assert all(BANK2[ORDER.index(c)] == 2 + c % 2 for c in range(STAY, CHUNKS))


def program(nc, x, adj, x2, eps1, eps2, W1, b1, W2, b2, Wm, bm, W, b, out, y_dram, part_dram):
    N, D = x.shape
    G = 16
    CH = N // (32 * G)
    TB = 4
    UN = CH // 2
    UC = N // UN // 4
    T1 = 3
    assert D == P and UC == 256 and CH == CHUNKS

    A_v = adj.rearrange("(u g h i) (v a k) -> u h v a i g k", u=UN, g=G, h=2, i=32, v=UN, a=4)
    x_stage = [t.rearrange("(v a t j) d -> v a j t d", v=UN, a=4, t=8, j=32) for t in (x, x2)]
    y_v = y_dram.rearrange("(u a b h j) d -> u h a j b d", u=UN, a=4, b=TB, h=2, j=32)
    out_v = out.rearrange("(u a b h j) d -> u h a j b d", u=UN, a=4, b=TB, h=2, j=32)

    with ExitStack() as ctx:
        def sb(name, shape, dt=F32, c=ctx):
            return c.enter_context(nc.sbuf_tensor(name, shape, dt))

        def sem(name):
            return ctx.enter_context(nc.semaphore(name))

        Sh = sb("S_hi", [P, CH, TB, D], F32R)
        Sl = sb("S_lo", [P, CH, TB, D], F32R)
        S32 = sb("S_plain", [P, 2, TB, D])
        with ExitStack() as same:
            hid_hi = sb("hidden_hi", [P, 2, TB * P], F32R, same)
        hid = sb("hidden", [P, 2, TB * P])
        WT_hi = sb("mlp_T_hi", [P, 2 * LAYERS, P], F32R)
        WT = sb("weights_T", [P, 3, P])
        ident_r = sb("ident", [P, P], F32R)
        quad_sum = sb("quad_sum", [P, P])
        bm_row = sb("bm_row", [P, D])
        b_row = sb("b_row", [P, D])
        bT = sb("bias_T", [P, 2 * LAYERS])
        ax_scale = sb("ax_scale", [P, 2])
        deg_part = sb("deg_part", [P, UN, G])
        deg_quad = sb("deg_quad", [P, G])
        deg = sb("deg", [P, TB])
        deg_zero = sb("deg_zero", [P, TB])
        deg_pow = sb("deg_pow", [P, TB])
        dinv = sb("dinv", [P, TB])
        dinv_all = sb("dinv_all", [P, CH, TB])
        stats = sb("stats", [P, TB, 6])
        mean = sb("mean", [P, TB])
        mean_diff = sb("mean_diff", [P, TB])
        var_eps = sb("var_eps", [P, TB])
        rstd = sb("rstd", [P, TB])
        minus_half = sb("minus_half", [P, TB])
        R = sb("A_rows", [P, 2, G, UC])
        T = sb("A_cols", [P, T1, TB, G, 32])
        H = sb("A_hi", [P, 2, TB, G * 32], F32R)
        L = sb("A_lo", [P, 2, TB, G * 32], F32R)
        with ExitStack() as first:
            WT_lo = sb("mlp_T_lo", [P, 2 * LAYERS, P], F32R, first)
            hid_lo = sb("hidden_lo", [P, 2, TB * P], F32R, first)
            sb("pad", [P, 2 * P], F32, first)
            Xh1 = sb("x_hi", [P, CH, TB, D], F32R, first)
            Xl1 = sb("x_lo", [P, CH, TB, D], F32R, first)
            Xh2 = sb("x2_hi", [P, CH, TB, D], F32R, first)
            Xl2 = sb("x2_lo", [P, CH, TB, D], F32R, first)
        Xh, Xl = (Xh1, Xh2), (Xl1, Xl2)
        T_late = sb("A_cols_late", [P, TB, G, 32])
        H2 = sb("A_hi_2", [P, TB, G * 32], F32R)
        yz_a = sb("y_z_a", [P, 2, TB, D])
        S32_late = sb("S_plain_late", [P, TB, D])
        part_in0 = sb("part_in0", [P, TB * P])
        L2 = sb("A_lo_2", [P, TB, G * 32], F32R)
        yz_b = sb("y_z_b", [P, 2, TB, D])
        part_in1 = sb("part_in1", [P, TB * P])
        part_in2 = sb("part_in2", [P, TB * P])
        R2 = sb("A_rows_2", [P, G, UC])
        T2 = sb("A_cols_2", [P, 2, TB, G, 32])

        ident = ident_r[:].bitcast(F32)
        yt = S32[:, 1].rearrange("p b d -> p (b d)")
        z_last = hid[:, 1].rearrange("p (b d) -> p b d", b=TB)
        yt_last = hid[:, 0]
        plain_S = dict(zip(PLAIN, (S32_late[:], S32[:, 1], S32[:, 0])))
        part_in = [part_in1, part_in0, part_in2]
        PI = len(part_in)
        yz = [yz_a[:, 0], yz_a[:, 1], yz_b[:, 0], yz_b[:, 1]]
        YZ = len(yz)
        r0, h0 = len(UNITS1) % 2, TILES % 2
        R_slot = [R[:, r0], R[:, 1 - r0], R2[:]]
        T_slot = [T[:, (TILES + i) % T1] for i in range(T1)] + [T2[:, 0], T2[:, 1], T_late[:]]
        H_slot = [H[:, h0], H[:, 1 - h0], H2[:]]
        L_slot = [L[:, h0], L[:, 1 - h0], L2[:]]
        SLOTS, RS, TS = len(H_slot), len(R_slot), len(T_slot)

        bank = [ctx.enter_context(nc.psum_tensor(f"bank{i}", [P, 512], F32)) for i in range(8)]
        acc, acc_S, hidp, V, U = bank[0:2], bank[2:4], bank[4:6], bank[6], bank[7]

        rows_in1 = [sem(f"rows_in1_{i}") for i in range(2)]
        first_in, first_t = sem("first_in"), sem("first_t")
        rows_in2 = [sem(f"rows_in2_{i}") for i in range(RS)]
        x_in = [[sem(f"x{t + 1}_in{v}") for v in range(UN)] for t in range(2)]
        weights_in = sem("weights_in")
        consts_in = sem("consts_in")
        xh_done, xl_done = sem("xh_done"), sem("xl_done")
        masks = sem("masks")
        scale_ready = sem("scale_ready")
        wt_done, wt_ready, wt_low = sem("wt_done"), sem("wt_ready"), sem("wt_low")
        t_done, deg_half = sem("t_done"), sem("deg_half")
        h_done, l_done = sem("h_done"), sem("l_done")
        h_used, l_used, t_used = sem("h_used"), sem("l_used"), sem("t_used")
        acc1_done = sem("acc1_done")
        hid_val, hid_ready, hid_low, hid_done = sem("hid_val"), sem("hid_ready"), sem("hid_low"), sem("hid_done")
        deg_cols, deg_summed = sem("deg_cols"), sem("deg_summed")
        merged = sem("merged")
        norm_step, pow_done, y_done = sem("norm_step"), sem("pow_done"), sem("y_done")
        yt_done, yt_ready, support = sem("yt_done"), sem("yt_ready"), sem("support")
        s_step, sh_done, sl_done, yp_done = sem("s_step"), sem("sh_done"), sem("sl_done"), sem("yp_done")
        y_stored, plain_ready = sem("y_stored"), sem("plain_ready")
        part_taken, part_stored, part_used = sem("part_taken"), sem("part_stored"), sem("part_used")
        part_back = [sem(f"part_back{i}") for i in range(PI)]
        prod_ready, prod_t = sem("prod_ready"), sem("prod_t")
        y_back = [sem(f"y_back{i}") for i in range(YZ)]
        norm2_step, pow2_done, out_ready = sem("norm2_step"), sem("pow2_done"), sem("out_ready")
        stored = [sem(f"stored{i}") for i in range(YZ)]
        RELU_AT = (2, 3, 4)
        LOW_AT, LOW2_AT = (1, 3, 4), (2, 4, 6)
        HID = 2 * (LAYERS + 1)
        WT_PARTS = [(0, 4), (4, 6)]
        NORM, SSTEP, NORM2 = 11, 2, 5

        wT_bank = acc_S
        x_stage_buf = [hid[:].rearrange("p t (s d) -> p (t s) d", d=D),
                       S32[:].rearrange("p t s d -> p (t s) d")]
        t_late = T_late[:].rearrange("p t g i -> p (t g i)").rearrange("p (t s d) -> p t s d", t=2, d=D)
        stage = [x_stage_buf, [t_late[:, 0], t_late[:, 1]], x_stage_buf, x_stage_buf]
        w_stage = hid[:].rearrange("p t (s d) -> p (t s) d", d=D)
        w_last = S32[:, 0, 0, :]
        biases = S32[0:2 * LAYERS, 0, 1, :]

        def split_no(m):
            return sum(SPLIT[:m])

        def slot_free(eng, m, used):
            s = split_no(m)
            if s < 2:
                eng.wait_ge(used, TILES - 1 + s)
            elif s < SLOTS:
                eng.wait_ge(l_used, TILES)
            else:
                eng.wait_ge(used, TILES + s - SLOTS + 1)

        def tile_used(eng, m):
            if SPLIT[m]:
                eng.wait_ge(l_used, TILES + split_no(m) + 1)
            else:
                eng.wait_ge(t_used, m + 1 - split_no(m))

        def sums_before(n):
            return sum(i is not None for _, i, _, _ in TILES1[:n])

        def unit_free1(eng, unit):
            last = UNITS1[unit][2]
            if TILES1[last][1] is None:
                eng.wait_ge(t_done, last + 1)
            else:
                eng.wait_ge(deg_half, sums_before(last + 1))

        block = ctx.enter_context(nc.Block())

        @block.sync
        def _(sp):
            def load_rows(dst, c, v, signal):
                for a in range(4):
                    sp.dma_start(dst[32 * a:32 * a + 32], A_v[c // 2, c % 2, v, a]).then_inc(signal, 16)

            def load_rows1(n):
                load_rows(R[:, n % 2], UNITS1[n][0], UNITS1[n][1], rows_in1[n % 2])

            def load_x(v, ts=(0, 1)):
                for t in ts:
                    for a in range(4):
                        sp.dma_start(stage[v][t][32 * a:32 * a + 32], x_stage[t][v, a]).then_inc(x_in[t][v], 16)

            def load_weights():
                for t, w in enumerate((W1, W2)):
                    sp.dma_start(w_stage[:, 3 * t:3 * t + 3, :], w.rearrange("l e d -> e l d")).then_inc(weights_in, 16)
                sp.dma_start(w_stage[:, 6:8, :], Wm.rearrange("e (s d) -> e s d", s=2)).then_inc(weights_in, 16)
                sp.dma_start(w_last, W).then_inc(weights_in, 16)
                for t, bias in enumerate((b1, b2)):
                    sp.dma_start(biases[LAYERS * t:LAYERS * t + LAYERS], bias).then_inc(weights_in, 16)

            load_x(0, [0])
            for half in range(2):
                for a in range(4):
                    sp.dma_start(R[32 * a:32 * a + 32, 0, 8 * half:8 * half + 8],
                                 A_v[0, 0, 0, a][:, 8 * half:8 * half + 8]).then_inc(first_in if half == 0 else rows_in1[0], 16)
            load_x(0, [1])
            load_rows1(1)
            load_x(1)
            sp.wait_ge(deg_half, 2)
            load_rows1(2)
            sp.wait_ge(xl_done, 2)
            load_x(2)
            sp.wait_ge(deg_half, 4)
            load_rows1(3)
            sp.wait_ge(xl_done, 6)
            load_x(3)
            unit_free1(sp, UN - 2)
            load_rows1(UN)
            sp.wait_ge(xl_done, 8)
            load_weights()
            for n in range(UN + 1, len(UNITS1)):
                unit_free1(sp, n - 2)
                load_rows1(n)

            for n, (c, v) in enumerate(UNITS2):
                if n < 2:
                    unit_free1(sp, len(UNITS1) - 2 + n)
                elif n < RS:
                    sp.wait_ge(l_used, TILES)
                else:
                    sp.wait_ge(t_done, TILES + LAST_OF_UNIT[n - RS] + 1)
                load_rows(R_slot[n % RS], c, v, rows_in2[n % RS])

        @block.gpsimd
        def _(pool):
            nc.gpsimd.memset(ident, 0.0).then_inc(masks, 1)
            nc.gpsimd.memset(quad_sum[:], 0.0).then_inc(masks, 1)
            nc.gpsimd.memset(minus_half[:], -0.5).then_inc(masks, 1)
            pool.wait_ge(masks, 2)
            nc.gpsimd.affine_select(out=ident_r[:], in_=ident, compare_op=ALU.not_equal, fill=1.0, base=0,
                                    pattern=[[-1, P]], channel_multiplier=1).then_inc(masks, 1)
            for s in range(-3, 4):
                nc.gpsimd.affine_select(out=quad_sum[:], in_=quad_sum[:], compare_op=ALU.not_equal, fill=1.0,
                                        base=32 * s, pattern=[[-1, P]], channel_multiplier=1).then_inc(masks, 1)
                pool.wait_ge(masks, 8 + s)

            def low(dst, t, hi):
                return nc.gpsimd.tensor_tensor(dst.rearrange("p t n -> p (t n)"),
                                               t.rearrange("p t g i -> p (t g i)"),
                                               hi.rearrange("p t n -> p (t n)").bitcast(F32), ALU.subtract)

            def powers(pc):
                pool.wait_ge(norm_step, NORM * pc + NORM - 1)
                nc.gpsimd.tensor_tensor(rstd[:], var_eps[:], minus_half[:], ALU.pow).then_inc(pow_done, 1)
                nc.gpsimd.tensor_tensor(deg_pow[:], deg[:], minus_half[:], ALU.pow).then_inc(pow_done, 1)

            for n, (c, i, _, _) in enumerate(TILES1):
                pool.wait_ge(h_done, n + 1)
                if n >= 2:
                    pool.wait_ge(l_used, n - 1)
                low(L[:, n % 2], T[:, n % T1], H[:, n % 2]).then_inc(l_done, 1)
                if i == 6 and c > 0:
                    powers(c - 1)

            def powers2(j):
                pool.wait_ge(norm2_step, NORM2 * j + NORM2)
                nc.gpsimd.tensor_tensor(rstd[:], var_eps[:], minus_half[:], ALU.pow).then_inc(pow2_done, 1)

            for m in range(POSTS_END):
                if m < M and SPLIT[m]:
                    s = split_no(m)
                    pool.wait_ge(h_done, TILES + s + 1)
                    slot_free(pool, m, l_used)
                    low(L_slot[s % SLOTS], T_slot[T_OF[m]], H_slot[s % SLOTS]).then_inc(l_done, 1)
                if m == 8:
                    powers(CH - 1)
                if m in NORM_AT:
                    powers2(NORM_AT.index(m))

        @block.scalar
        def _(act):
            nc_act = nc.scalar

            def load_consts():
                act.dma_start(bm_row[:], bm.rearrange("(o d) -> o d", o=1).to_broadcast([P, D])).then_inc(consts_in, 16)
                act.dma_start(b_row[:], b.rearrange("(o d) -> o d", o=1).to_broadcast([P, D])).then_inc(consts_in, 16)
                for t, e in enumerate((eps1, eps2)):
                    act.dma_start(ax_scale[:, t:t + 1], e.rearrange("(o d) -> o d", o=1).to_broadcast([P, 1])).then_inc(consts_in, 16)
            def x_high(v, t):
                act.wait_ge(x_in[t][v], 64)
                dst = Xh[t][:, 2 * v:2 * v + 2].rearrange("p h b d -> p b h d")
                nc_act.activation(dst, stage[v][t].rearrange("p (b h) d -> p b h d", h=2), ACT.Copy).then_inc(xh_done, 1)

            def high(dst, t):
                return nc_act.activation(dst.rearrange("p t n -> p (t n)"), t.rearrange("p t g i -> p (t g i)"), ACT.Copy)

            def take_ax(pc, t):
                if t == 0:
                    act.wait_ge(acc1_done, pc + 1)
                    if pc == 0:
                        act.wait_ge(scale_ready, 1)
                    else:
                        act.wait_ge(hid_ready, HID * pc)
                else:
                    act.wait_ge(l_used, END1[pc])
                nc_act.activation(hidp[t][:], acc[t][:], ACT.Copy, scale=ax_scale[:, t:t + 1]).then_inc(hid_val, 1)

            def hid_high(pc, layer):
                if layer == 0 and pc == 0:
                    act.wait_ge(wt_done, 1)
                elif layer == 0:
                    act.wait_ge(merged, pc)
                for t in range(2):
                    act.wait_ge(hid_val, 2 * LAYERS * pc + 2 * layer + t + 1)
                    nc_act.activation(hid_hi[:, t], hidp[t][:], ACT.Copy).then_inc(hid_ready, 1)

            def take_part(pc):
                act.wait_ge(l_used, END1[pc // 2 * 2 + 1])
                act.wait_ge(support, pc // 2 * 2 + 1)
                if pc > LAG:
                    act.wait_ge(part_stored, 16 * (pc - LAG))
                nc_act.activation(yt, acc_S[pc % 2][:], ACT.Copy).then_inc(part_taken, 1)

            def store_part(pc):
                act.wait_ge(part_taken, pc - LAG + 1)
                act.dma_start(part_dram[pc], yt).then_inc(part_stored, 16)

            def relu(pc, layer):
                for t in range(2):
                    act.wait_ge(hid_done, 2 * LAYERS * pc + 2 * layer + t + 1)
                    i = LAYERS * t + layer
                    if layer < LAYERS - 1:
                        nc_act.activation(hidp[t][:], hidp[t][:], ACT.Relu, bias=bT[:, i:i + 1]).then_inc(hid_val, 1)
                    else:
                        nc_act.activation(hid[:, t].rearrange("p (b a i) -> p a b i", a=4, b=TB),
                                          hidp[t][:].rearrange("p (a b i) -> p a b i", a=4, b=TB),
                                          ACT.Relu, bias=bT[:, i:i + 1]).then_inc(hid_ready, 1)
                if layer < LAYERS - 1:
                    hid_high(pc, layer + 1)

            def take_yt(pc, dst):
                act.wait_ge(yt_done, pc + 1)
                if pc > 0:
                    act.wait_ge(support, pc)
                if pc % 2 == 1 and LAG <= pc < STAY:
                    act.wait_ge(part_stored, 16 * (pc - LAG + 1))
                nc_act.activation(dst, U[:], ACT.Copy).then_inc(yt_ready, 1)

            def s_high(pc):
                act.wait_ge(s_step, SSTEP * pc + 2)
                nc_act.activation(Sh[:, pc], V[:].rearrange("p (b d) -> p b d", b=TB), ACT.Copy).then_inc(sh_done, 1)

            def store_y(pc, src):
                act.wait_ge(yp_done, pc + 1)
                for a in range(4):
                    act.dma_start(y_v[pc // 2, pc % 2, a], src[32 * a:32 * a + 32]).then_inc(y_stored, 16)

            for n, (c, i, _, _) in enumerate(TILES1):
                pc = c - 1
                parts = c % 2 == 0 and c > LAG
                if c == 0 and i % 2 == 0:
                    x_high(i // 2, 0)
                if n == 0:
                    for half in range(2):
                        act.wait_ge(t_done if half else first_t, 1)
                        rows = slice(8 * half, 8 * half + 8)
                        last = nc_act.activation(H[:, 0].rearrange("p t (g i) -> p t g i", g=G)[:, :, rows],
                                                 T[:, 0, :, rows], ACT.Copy)
                    last.then_inc(h_done, 1)
                else:
                    act.wait_ge(t_done, n + 1)
                    if n >= 2:
                        act.wait_ge(h_used, n - 1)
                        act.wait_ge(l_done, n - 1)
                    high(H[:, n % 2], T[:, n % T1]).then_inc(h_done, 1)
                if c == 0:
                    if i % 2 == 0:
                        x_high(i // 2, 1)
                    if i == 2:
                        load_consts()
                    continue
                if i == 0:
                    take_ax(pc, 0)
                    take_ax(pc, 1)
                    hid_high(pc, 0)
                    if c == 1:
                        for k, (first, end) in enumerate(WT_PARTS):
                            nc_act.activation(WT_hi[:, first:end].rearrange("p s d -> p (s d)"),
                                              wT_bank[k][:, 0:P * (end - first)], ACT.Copy).then_inc(wt_ready, 1)
                        nc_act.activation(WT[:, 0:2].rearrange("p s d -> p (s d)"), wT_bank[1][:, 2 * P:], ACT.Copy).then_inc(wt_ready, 1)
                        nc_act.activation(WT[:, 2], V[:, 0:P], ACT.Copy).then_inc(wt_ready, 1)
                        nc_act.activation(bT[:], V[:, P:P + 2 * LAYERS], ACT.Copy).then_inc(wt_ready, 1)
                        act.wait_ge(wt_ready, 5)
                    if pc > 0:
                        take_yt(pc - 1, yt)
                if i == 1 and parts:
                    take_part(c - 2)
                if i == 2:
                    if pc > 0:
                        s_high(pc - 1)
                    if parts:
                        store_part(c - 2)
                if i in RELU_AT:
                    relu(pc, RELU_AT.index(i))
                if i == 4:
                    if parts:
                        take_part(c - 1)
                    if pc > 0:
                        store_y(pc - 1, S32[:, 0])
                if i == 5 and parts:
                    store_part(c - 1)

            def take_prod(j):
                tile_used(act, LAST[j])
                if j == 0:
                    act.wait_ge(support, CH)
                elif j == 1:
                    act.wait_ge(y_stored, 64 * CH)
                else:
                    act.wait_ge(prod_t, j - 1)
                nc_act.activation(hid[:, j % 2].rearrange("p (b a i) -> p a b i", a=4, b=TB),
                                  bank[BANK2[j]][:].rearrange("p (a b i) -> p a b i", a=4, b=TB), ACT.Copy).then_inc(prod_ready, 1)

            def load_y(j):
                k = ORDER[j]
                if j < YZ:
                    act.wait_ge(l_used, TILES)
                else:
                    act.wait_ge(stored[j % YZ], 64 * (j // YZ))
                act.wait_ge(y_stored, 64 * k + 64)
                for a in range(4):
                    act.dma_start(yz[j % YZ][32 * a:32 * a + 32], y_v[k // 2, k % 2, a]).then_inc(y_back[j % YZ], 16)

            def load_part(i):
                if i == 0:
                    act.wait_ge(l_used, TILES)
                elif i < PI:
                    act.wait_ge(norm_step, NORM * CH - 5)
                else:
                    act.wait_ge(part_used, i - PI + 1)
                act.wait_ge(part_stored, 16 * (ORDER[BACK[i]] - LAG + 1))
                act.dma_start(part_in[i % PI][:], part_dram[ORDER[BACK[i]]]).then_inc(part_back[i % PI], 16)

            def store_out(j):
                k = ORDER[j]
                act.wait_ge(out_ready, j + 1)
                for a in range(4):
                    act.dma_start(out_v[k // 2, k % 2, a], yz[j % YZ][32 * a:32 * a + 32]).then_inc(stored[j % YZ], 16)

            for m in range(POSTS_END):
                if m < M and SPLIT[m]:
                    act.wait_ge(t_done, TILES + m + 1)
                    slot_free(act, m, h_used)
                    slot_free(act, m, l_done)
                    high(H_slot[split_no(m) % SLOTS], T_slot[T_OF[m]]).then_inc(h_done, 1)
                if m == 0:
                    take_ax(CH - 1, 0)
                    take_ax(CH - 1, 1)
                    hid_high(CH - 1, 0)
                    take_yt(CH - 2, yt)
                if m == 3:
                    s_high(CH - 2)
                    relu(CH - 1, 0)
                if m == 5:
                    relu(CH - 1, 1)
                    store_y(CH - 2, S32[:, 0])
                if m == 6:
                    relu(CH - 1, 2)
                if m == 10:
                    take_yt(CH - 1, yt_last)
                if m == 13:
                    s_high(CH - 1)
                if m == 15:
                    store_y(CH - 1, z_last)
                for j in range(CHUNKS):
                    if m == TAKE_AT[j]:
                        take_prod(j)
                    if m == LOAD_Y_AT[j]:
                        load_y(j)
                    if m == STORE_AT[j]:
                        store_out(j)
                for i in range(len(BACK)):
                    if m == LOAD_PART_AT[i]:
                        load_part(i)
            for i in range(YZ):
                act.wait_ge(stored[i], 64 * CH // YZ)

        @block.vector
        def _(dve):
            def transpose_tile(dst, half, src):
                return nc.vector.transpose(dst, src.rearrange("p g (b h j) -> p h b g j", h=2, j=32)[:, half])

            def x_low(v, t):
                dve.wait_ge(xh_done, 2 * v + t + 1)
                hi = Xh[t][:, 2 * v:2 * v + 2].rearrange("p h b d -> p b h d").bitcast(F32)
                lo = Xl[t][:, 2 * v:2 * v + 2].rearrange("p h b d -> p b h d")
                nc.vector.tensor_tensor(lo, stage[v][t].rearrange("p (b h) d -> p b h d", h=2), hi,
                                        ALU.subtract).then_inc(xl_done, 1)

            def hid_low_part(pc, layer):
                for t in range(2):
                    dve.wait_ge(hid_ready, HID * pc + 2 * layer + t + 1)
                    nc.vector.tensor_tensor(hid_lo[:, t], hidp[t][:], hid_hi[:, t].bitcast(F32),
                                            ALU.subtract).then_inc(hid_low, 1)

            def steps(signal, base):
                count = [0]

                def step(ins):
                    count[0] += 1
                    ins.then_inc(signal, 1)
                    dve.wait_ge(signal, base + count[0])
                return step

            def moments_of(z, step):
                for i in range(TB):
                    last = nc.vector.bn_stats(stats[:, i], z[:, i])
                step(last)
                even, odd = stats[:, :, 0:3], stats[:, :, 3:6]
                nc.vector.tensor_tensor(mean[:], even[:, :, 1], odd[:, :, 1], ALU.add)
                nc.vector.tensor_tensor(mean_diff[:], even[:, :, 1], odd[:, :, 1], ALU.subtract)
                step(nc.vector.tensor_tensor(var_eps[:], even[:, :, 2], odd[:, :, 2], ALU.add))
                nc.vector.tensor_scalar(mean[:], mean[:], 0.5, None, ALU.mult)
                nc.vector.tensor_tensor(mean_diff[:], mean_diff[:], mean_diff[:], ALU.mult)
                step(nc.vector.tensor_scalar(var_eps[:], var_eps[:], 1.0 / D, LN_EPS, ALU.mult, ALU.add))
                step(nc.vector.scalar_tensor_tensor(var_eps[:], mean_diff[:], 0.25, var_eps[:], ALU.mult, ALU.add))

            def norm1(pc, z):
                step = steps(norm_step, NORM * pc)
                dve.wait_ge(deg_summed, pc + 1)
                for a in range(4):
                    last = nc.vector.tensor_scalar(deg[32 * a:32 * a + 32], U[32 * a:32 * a + 32, 4 * a:4 * a + 4],
                                                   1.0, None, ALU.add)
                step(last)
                step(nc.vector.tensor_scalar(deg_zero[:], deg[:], 0.0, None, ALU.is_equal))
                step(nc.vector.tensor_tensor(deg[:], deg[:], deg_zero[:], ALU.add))
                dve.wait_ge(merged, pc + 1)
                if pc > 0:
                    dve.wait_ge(y_stored, 64 * pc)
                step(nc.vector.tensor_tensor(z, V[:].rearrange("p (b d) -> p b d", b=TB),
                                             bm_row[:].unsqueeze(1).to_broadcast([P, TB, D]), ALU.add))
                step(nc.vector.tensor_tensor(z, z, Xh1[:, pc].bitcast(F32), ALU.add))
                step(nc.vector.tensor_tensor(z, z, Xl1[:, pc].bitcast(F32), ALU.add))
                moments_of(z, step)

            def norm1_end(pc, z):
                dve.wait_ge(pow_done, 2 * pc + 2)
                nc.vector.tensor_tensor(dinv[:], deg_pow[:], deg_zero[:], ALU.subtract).then_inc(norm_step, 1)
                for i in range(TB):
                    last = nc.vector.tensor_scalar(z[:, i], z[:, i], mean[:, i:i + 1], rstd[:, i:i + 1],
                                                   ALU.subtract, ALU.mult)
                last.then_inc(y_done, 1)
                dve.wait_ge(norm_step, NORM * pc + NORM)
                nc.vector.tensor_copy(dinv_all[:, pc], dinv[:])

            v4 = V[:].rearrange("p (b d) -> p b d", b=TB)

            def support_scale(pc):
                step = steps(s_step, SSTEP * pc)
                dve.wait_ge(support, pc + 1)
                step(nc.vector.tensor_tensor(v4, v4, b_row[:].unsqueeze(1).to_broadcast([P, TB, D]), ALU.add))
                for i in range(TB):
                    last = nc.vector.tensor_scalar(v4[:, i], v4[:, i], dinv[:, i:i + 1], None, ALU.mult)
                last.then_inc(s_step, 1)

            def support_end(pc, z):
                dve.wait_ge(sh_done, pc + 1)
                nc.vector.tensor_tensor(Sl[:, pc], v4, Sh[:, pc].bitcast(F32), ALU.subtract).then_inc(sl_done, 1)
                dve.wait_ge(y_done, pc + 1)
                for i in range(TB):
                    last = nc.vector.scalar_tensor_tensor(z[:, i], v4[:, i], dinv[:, i:i + 1], z[:, i], ALU.mult, ALU.add)
                last.then_inc(yp_done, 1)

            for n, (c, i, _, q) in enumerate(TILES1):
                unit = UNIT_OF1[n]
                rows = R[:, unit % 2]
                if n == 0:
                    x_low(0, 0)
                if n == 0:
                    dve.wait_ge(first_in, 64)
                    transpose_tile(T[:, 0, :, 0:G // 2], 0, rows[:, 0:G // 2]).then_inc(first_t, 1)
                    dve.wait_ge(rows_in1[0], 64)
                    transpose_tile(T[:, 0, :, G // 2:], 0, rows[:, G // 2:]).then_inc(t_done, 1)
                else:
                    dve.wait_ge(rows_in1[unit % 2], 64 * (unit // 2 + 1))
                    if n >= T1:
                        dve.wait_ge(l_done, n - T1 + 1)
                    transpose_tile(T[:, n % T1], q % 2, rows).then_inc(t_done, 1)
                if i is None:
                    continue
                if c == 0 and i > 0 and i % 2 == 0:
                    x_low(i // 2, 0)
                if c == 0 and i == 6:
                    dve.wait_ge(consts_in, 64)
                    nc.vector.tensor_scalar(ax_scale[:], ax_scale[:], 1.0, 1.0, ALU.add, ALU.add).then_inc(scale_ready, 1)
                if c > 0 and i == 0:
                    dve.wait_ge(deg_cols, c)
                if n == 1:
                    x_low(0, 1)
                if n > 0:
                    for half in ([0, 1] if n == 1 else [i % 2]):
                        part = slice(8 * half, 8 * half + 8)
                        nc.vector.tensor_reduce(deg_part[:, i // 2, part], rows[:, part], AX.X, ALU.add).then_inc(deg_half, 1)
                if c == 0 and i > 0 and i % 2 == 0:
                    x_low(i // 2, 1)
                if c == 1 and i == 1:
                    dve.wait_ge(wt_ready, 5)
                    for k, (first, end) in enumerate(WT_PARTS):
                        nc.vector.tensor_tensor(WT_lo[:, first:end].rearrange("p s d -> p (s d)"),
                                                wT_bank[k][:, 0:P * (end - first)],
                                                WT_hi[:, first:end].rearrange("p s d -> p (s d)").bitcast(F32),
                                                ALU.subtract).then_inc(wt_low, 1)
                if c > 0 and i in LOW_AT:
                    hid_low_part(c - 1, LOW_AT.index(i))
                if c >= 2 and i == 2:
                    support_scale(c - 2)
                if c >= 2 and i == 3:
                    support_end(c - 2, S32[:, 0])
                if c > 0 and i == 6:
                    norm1(c - 1, S32[:, 0])
                if c > 0 and i == 7:
                    norm1_end(c - 1, S32[:, 0])
                if i == 7:
                    if c > 0:
                        dve.wait_ge(deg_summed, c)
                    dve.wait_ge(deg_half, CH * c + CH)
                    nc.vector.tensor_reduce(deg_quad[:], deg_part[:].rearrange("p u g -> p g u"), AX.X,
                                            ALU.add).then_inc(deg_cols, 1)

            def plain(i):
                q = PLAIN[i]
                nc.vector.tensor_tensor(plain_S[q], Sh[:, q].bitcast(F32), Sl[:, q].bitcast(F32),
                                        ALU.add).then_inc(plain_ready, 1)

            def norm2(j):
                z, k = yz[j % YZ], ORDER[j]
                u4 = U[:].rearrange("p (b d) -> p b d", b=TB)
                step = steps(norm2_step, NORM2 * j)
                dve.wait_ge(prod_t, j + 1)
                dve.wait_ge(y_back[j % YZ], 64 * (j // YZ + 1))
                for i in range(TB):
                    last = nc.vector.scalar_tensor_tensor(z[:, i], u4[:, i], dinv_all[:, k, i:i + 1], z[:, i],
                                                          ALU.mult, ALU.add)
                step(last)
                moments_of(z, step)

            def norm2_end(j):
                z = yz[j % YZ]
                dve.wait_ge(pow2_done, j + 1)
                for i in range(TB):
                    last = nc.vector.tensor_scalar(z[:, i], z[:, i], mean[:, i:i + 1], rstd[:, i:i + 1],
                                                   ALU.subtract, ALU.mult)
                last.then_inc(out_ready, 1)

            for m in range(POSTS_END):
                if m < M:
                    n = UNIT_OF[m]
                    dve.wait_ge(rows_in2[n % RS], 64 * (n // RS + 1))
                    if m < T1:
                        dve.wait_ge(l_done, TILES - T1 + 1 + m)
                    elif T_OF[m] not in T_OF[:m]:
                        dve.wait_ge(l_used, TILES)
                        if T_OF[m] == TS - 1:
                            dve.wait_ge(hid_done, 2 * LAYERS * CH)
                    else:
                        back = max(k for k in range(m) if T_OF[k] == T_OF[m])
                        if SPLIT[back]:
                            dve.wait_ge(l_done, TILES + split_no(back) + 1)
                        else:
                            tile_used(dve, back)
                    transpose_tile(T_slot[T_OF[m]], TILES2[m][1] % 2, R_slot[n % RS]).then_inc(t_done, 1)
                if m in LOW2_AT:
                    hid_low_part(CH - 1, LOW2_AT.index(m))
                if m == 2:
                    dve.wait_ge(l_used, TILES)
                    plain(0)
                if m == 3:
                    support_scale(CH - 2)
                    plain(1)
                if m == 4:
                    support_end(CH - 2, S32[:, 0])
                if m == 9:
                    norm1(CH - 1, z_last)
                if m == 10:
                    norm1_end(CH - 1, z_last)
                if m == 13:
                    support_scale(CH - 1)
                if m == 14:
                    support_end(CH - 1, z_last)
                    dve.wait_ge(sl_done, CH)
                    dve.wait_ge(y_stored, 64 * (CH - 1))
                    plain(2)
                if m in NORM_END_AT:
                    norm2_end(NORM_END_AT.index(m))
                if m in NORM_AT:
                    norm2(NORM_AT.index(m))

        @block.tensor
        def _(pe):
            mm = nc.tensor.matmul

            def transpose_weights():
                pe.wait_ge(weights_in, 96)
                pe.wait_ge(masks, 11)
                for i in range(8):
                    nc.tensor.transpose(wT_bank[i // 4][:, P * (i % 4):P * (i % 4) + P], w_stage[:, i], ident)
                nc.tensor.transpose(V[:, 0:P], w_last, ident)
                nc.tensor.transpose(V[:, P:P + 2 * LAYERS], biases, ident_r[0:2 * LAYERS, 0:2 * LAYERS].bitcast(F32)).then_inc(wt_done, 1)

            def layer(pc, i):
                if i == 0 and pc == 0:
                    pe.wait_ge(wt_low, 2)
                for t in range(2):
                    pe.wait_ge(hid_ready, HID * pc + 2 * i + t + 1)
                    pe.wait_ge(hid_low, 2 * LAYERS * pc + 2 * i + t + 1)
                    w = LAYERS * t + i
                    mm(hidp[t][:], WT_hi[:, w], hid_hi[:, t], start=True, stop=False)
                    mm(hidp[t][:], WT_lo[:, w], hid_hi[:, t], start=False, stop=False)
                    mm(hidp[t][:], WT_hi[:, w], hid_lo[:, t], start=False, stop=True).then_inc(hid_done, 1)

            def degrees(pc):
                pe.wait_ge(deg_cols, pc + 1)
                if pc > 0:
                    pe.wait_ge(yt_ready, pc)
                mm(U[:, 0:G], quad_sum[:], deg_quad[:], start=True, stop=True).then_inc(deg_summed, 1)

            def merge(pc):
                pe.wait_ge(hid_ready, HID * (pc + 1))
                if pc > 0:
                    pe.wait_ge(yp_done, pc)
                for i in range(TB):
                    for t in range(2):
                        last = mm(V[:, P * i:P * i + P], hid[:, t, P * i:P * i + P], WT[:, t],
                                  start=t == 0, stop=t == 1)
                last.then_inc(merged, 1)

            def transpose_y(pc, z):
                pe.wait_ge(y_done, pc + 1)
                for i in range(TB):
                    last = nc.tensor.transpose(U[:, P * i:P * i + P], z[:, i], ident)
                last.then_inc(yt_done, 1)

            def supports(pc, yt):
                pe.wait_ge(yt_ready, pc + 1)
                for i in range(TB):
                    last = mm(V[:, P * i:P * i + P], yt[:, P * i:P * i + P], WT[:, 2], start=True, stop=True)
                last.then_inc(support, 1)

            for n, (c, i, rc, q) in enumerate(TILES1):
                there = i is None or q <= c - LAG
                x_too = i is not None
                pe.wait_ge(h_done, n + 1)
                for t in range(2 if x_too else 0):
                    if c == 0 and i % 2 == 0:
                        pe.wait_ge(xl_done, i + t + 1)
                    if i == 0 and c > 0:
                        pe.wait_ge(hid_val, 2 * LAYERS * (c - 1) + t + 1)
                    for kk in range(TB):
                        mm(acc[t][:], Xh[t][:, q, kk], H[:, n % 2, kk], start=i == 0 and kk == 0, stop=False)
                        last = mm(acc[t][:], Xl[t][:, q, kk], H[:, n % 2, kk], start=False, stop=False)
                if there:
                    pe.wait_ge(sh_done, q + 1)
                    pe.wait_ge(sl_done, q + 1)
                    if q == 0 and rc >= LAG + 2:
                        pe.wait_ge(part_taken, rc - LAG - 1)
                    for kk in range(TB):
                        mm(acc_S[rc % 2][:], Sh[:, q, kk], H[:, n % 2, kk], start=q == 0 and kk == 0, stop=False)
                        last = mm(acc_S[rc % 2][:], Sl[:, q, kk], H[:, n % 2, kk], start=False, stop=False)
                last.then_inc(h_used, 1)
                if c == 0:
                    if i == 7:
                        transpose_weights()
                elif x_too:
                    if i == 2:
                        degrees(c - 1)
                    if i in (1, 2, 3):
                        layer(c - 1, i - 1)
                    if i == 7:
                        transpose_y(c - 1, S32[:, 0])
                    if i == 0 and c > 1:
                        supports(c - 2, yt)
                pe.wait_ge(l_done, n + 1)
                for t in range(2 if x_too else 0):
                    for kk in range(TB):
                        last = mm(acc[t][:], Xh[t][:, q, kk], L[:, n % 2, kk], start=False, stop=i == 7 and kk == TB - 1)
                    if i == 7 and t == 0:
                        last.then_inc(acc1_done, 1)
                if there:
                    end = rc < STAY and q == groups2(rc)[0] - 1
                    for kk in range(TB):
                        last = mm(acc_S[rc % 2][:], Sh[:, q, kk], L[:, n % 2, kk], start=False,
                                  stop=end and kk == TB - 1)
                last.then_inc(l_used, 1)
                if i == 4 and c > 0:
                    merge(c - 1)

            def transpose_product(j):
                pe.wait_ge(prod_ready, j + 1)
                if j == 0:
                    pe.wait_ge(yt_ready, CH)
                else:
                    pe.wait_ge(norm2_step, NORM2 * (j - 1) + 1)
                for i in range(TB):
                    last = nc.tensor.transpose(U[:, P * i:P * i + P], hid[:, j % 2, P * i:P * i + P], ident)
                last.then_inc(prod_t, 1)

            def begin(j):
                if j < 2:
                    pe.wait_ge(hid_val, 2 * LAYERS * (CH - 1) + j + 1)
                    return
                if ORDER[j] >= STAY:
                    return
                i = BACK.index(j)
                if BEFORE[j] is None:
                    pe.wait_ge(hid_ready, HID * CH)
                else:
                    pe.wait_ge(prod_ready, BEFORE[j] + 1)
                pe.wait_ge(part_back[i % PI], 16 * (i // PI + 1))
                mm(bank[BANK2[j]][:], ident, part_in[i % PI][:], start=True, stop=False).then_inc(part_used, 1)

            for m in range(POSTS_END):
                if m < M:
                    k, q = TILES2[m]
                    j = ORDER.index(k)
                    if m in (0, FIRST_OF_GROUP[CH - 2]):
                        pe.wait_ge(sh_done, CH - 2 if m == 0 else CH - 1)
                        pe.wait_ge(sl_done, CH - 2 if m == 0 else CH - 1)
                    if m == FIRST[j]:
                        begin(j)
                    a = bank[BANK2[j]][:]
                    fresh = m == FIRST[j] and j < 2
                    if SPLIT[m]:
                        slot = split_no(m) % SLOTS
                        pe.wait_ge(h_done, TILES + split_no(m) + 1)
                        for kk in range(TB):
                            mm(a, Sh[:, q, kk], H_slot[slot][:, kk], start=fresh and kk == 0, stop=False)
                            last = mm(a, Sl[:, q, kk], H_slot[slot][:, kk], start=False, stop=False)
                        last.then_inc(h_used, 1)
                    else:
                        pe.wait_ge(t_done, TILES + m + 1)
                        if m == FIRST_OF_GROUP[q]:
                            pe.wait_ge(plain_ready, PLAIN.index(q) + 1)
                        for kk in range(TB):
                            last = mm(a, plain_S[q][:, kk], T_slot[T_OF[m]][:, kk].rearrange("p g i -> p (g i)"),
                                      start=False, stop=m == LAST[j] and kk == TB - 1)
                        last.then_inc(t_used, 1)
                if m == 0:
                    supports(CH - 2, yt)
                if m in (1, 3, 4):
                    layer(CH - 1, (1, 3, 4).index(m))
                if m == 4:
                    degrees(CH - 1)
                if m == 6:
                    merge(CH - 1)
                if m == 9:
                    transpose_y(CH - 1, z_last)
                if m == 10:
                    supports(CH - 1, yt_last)
                if m in TRANSPOSE_AT:
                    transpose_product(TRANSPOSE_AT.index(m))
                if m < M and SPLIT[m]:
                    pe.wait_ge(l_done, TILES + split_no(m) + 1)
                    for kk in range(TB):
                        last = mm(a, Sh[:, q, kk], L_slot[slot][:, kk], start=False, stop=False)
                    last.then_inc(l_used, 1)


_INS = ["x", "adj", "L0_gnn_x2", "L0_gnn_eps1", "L0_gnn_eps2", "L0_gnn_W1", "L0_gnn_b1", "L0_gnn_W2", "L0_gnn_b2",
        "L0_gnn_Wm", "L0_gnn_bm", "L1_gnn_W", "L1_gnn_b"]


def kernel(**inputs):
    import numpy as np
    import concourse.bacc as bacc
    from concourse.bass_utils import run_bass_kernel_spmd as run

    nc = bacc.Bacc("TRN2", target_bir_lowering=False, num_devices=1)
    arrays, args = {}, []
    for name in _INS:
        a = np.ascontiguousarray(inputs[name])
        arrays["in_" + name] = a
        args.append(nc.dram_tensor("in_" + name, a.shape, mybir.dt.from_np(a.dtype), kind="ExternalInput").ap())
    shape = inputs["x"].shape
    args.append(nc.dram_tensor("out_0", shape, F32, kind="ExternalOutput").ap())
    args.append(nc.dram_tensor("y_scratch", shape, F32, kind="Internal").ap())
    args.append(nc.dram_tensor("part_scratch", (STAY, P, 512), F32, kind="Internal").ap())
    program(nc, *args)
    return run(nc, [arrays], core_ids=[0]).results[0]["out_0"]
```
